# Optimizing a Trainium2 kernel written in Bass

```python
import numpy as np
import jax
import jax.numpy as jnp

def _softmax(x, axis=-1):
    return jax.nn.softmax(x, axis=axis)

def _gelu(x):
    return jax.nn.gelu(x, approximate=True)

def _silu(x):
    return jax.nn.silu(x)

def _sigmoid(x):
    return jax.nn.sigmoid(x)

def _layernorm(x, axis=-1, eps=1e-05):
    m = jnp.mean(x, axis=axis, keepdims=True)
    v = jnp.var(x, axis=axis, keepdims=True)
    return (x - m) / jnp.sqrt(v + eps)

def _scatter_add(tgt, idx, src, axis=0):
    return tgt.at[idx].add(src)

def _segment_sum(src, seg, n):
    return jax.ops.segment_sum(src, seg, n)
kernel_name = 'mk_seq_postln_d1_jaxref_r8_b49844'

def setup_inputs(seed: int=0):
    np.random.seed(seed)
    _w = jnp.asarray

    def _L0_attn_setup():
        import jax, jax.numpy as jnp
        import numpy as np
        import math
        B, L, D, H = (32, 64, 512, 32)
        HD = D // H
        key = jax.random.key(seed)
        ks = jax.random.split(key, 9)
        s = 1.0 / math.sqrt(D)
        return {'x': jax.random.normal(ks[0], (B, L, D), jnp.float32), 'Wq': jax.random.normal(ks[1], (D, D), jnp.float32) * s, 'bq': jax.random.normal(ks[2], (D,), jnp.float32) * s, 'Wk': jax.random.normal(ks[3], (D, D), jnp.float32) * s, 'bk': jax.random.normal(ks[4], (D,), jnp.float32) * s, 'Wv': jax.random.normal(ks[5], (D, D), jnp.float32) * s, 'bv': jax.random.normal(ks[6], (D,), jnp.float32) * s, 'Wo': jax.random.normal(ks[7], (D, D), jnp.float32) * s, 'bo': jax.random.normal(ks[8], (D,), jnp.float32) * s}
    _L0_attn_in = _L0_attn_setup()

    def _L0_ffn_setup():
        import jax, jax.numpy as jnp
        import numpy as np
        BLOCK = 64
        NF4_CODE = jnp.array([-1.0, -0.6961928009986877, -0.5250730514526367, -0.39491748809814453, -0.28444138169288635, -0.18477343022823334, -0.09105003625154495, 0.0, 0.07958029955625534, 0.16093020141124725, 0.24611230194568634, 0.33791524171829224, 0.44070982933044434, 0.5626170039176941, 0.7229568362236023, 1.0], dtype=jnp.float32)

        def dequant_nf4(q, absmax, shape):
            w = NF4_CODE[q.reshape(-1)]
            w = w.reshape(-1, BLOCK) * absmax[:, None]
            return w.reshape(shape)
        key = jax.random.key(seed)
        ks = jax.random.split(key, 7)
        HD, M = (512, 1792)
        nblk = HD * M // BLOCK
        x = jax.random.normal(ks[0], (2, 256, HD), dtype=jnp.float32)
        gate_q = jax.random.randint(ks[1], (M, HD), 0, 16, dtype=jnp.int32)
        up_q = jax.random.randint(ks[2], (M, HD), 0, 16, dtype=jnp.int32)
        down_q = jax.random.randint(ks[3], (HD, M), 0, 16, dtype=jnp.int32)
        gate_absmax = jax.random.uniform(ks[4], (nblk,), dtype=jnp.float32) * 0.05
        up_absmax = jax.random.uniform(ks[5], (nblk,), dtype=jnp.float32) * 0.05
        down_absmax = jax.random.uniform(ks[6], (nblk,), dtype=jnp.float32) * 0.05
        return {'x': x, 'gate_q': gate_q, 'gate_absmax': gate_absmax, 'up_q': up_q, 'up_absmax': up_absmax, 'down_q': down_q, 'down_absmax': down_absmax}
    _L0_ffn_in = _L0_ffn_setup()
    _d = {'L0_attn_x': _L0_attn_in['x'], 'L0_attn_Wq': _L0_attn_in['Wq'], 'L0_attn_bq': _L0_attn_in['bq'], 'L0_attn_Wk': _L0_attn_in['Wk'], 'L0_attn_bk': _L0_attn_in['bk'], 'L0_attn_Wv': _L0_attn_in['Wv'], 'L0_attn_bv': _L0_attn_in['bv'], 'L0_attn_Wo': _L0_attn_in['Wo'], 'L0_attn_bo': _L0_attn_in['bo'], 'L0_ffn_gate_q': _L0_ffn_in['gate_q'], 'L0_ffn_gate_absmax': _L0_ffn_in['gate_absmax'], 'L0_ffn_up_q': _L0_ffn_in['up_q'], 'L0_ffn_up_absmax': _L0_ffn_in['up_absmax'], 'L0_ffn_down_q': _L0_ffn_in['down_q'], 'L0_ffn_down_absmax': _L0_ffn_in['down_absmax']}
    _x0 = _d['L0_attn_x']
    _d['L0_attn_x'] = jax.random.normal(jax.random.fold_in(jax.random.key(seed), 1), (8, 256, 512), dtype=_x0.dtype)
    del _x0
    return _d

def reference(L0_attn_x, L0_attn_Wq, L0_attn_bq, L0_attn_Wk, L0_attn_bk, L0_attn_Wv, L0_attn_bv, L0_attn_Wo, L0_attn_bo, L0_ffn_gate_q, L0_ffn_gate_absmax, L0_ffn_up_q, L0_ffn_up_absmax, L0_ffn_down_q, L0_ffn_down_absmax):

    def _L0_attn_ref(x, Wq, bq, Wk, bk, Wv, bv, Wo, bo):
        import jax, jax.numpy as jnp
        import numpy as np
        import math
        B, L, D, H = (32, 64, 512, 32)
        HD = D // H
        b, l, d = x.shape
        h, hd = (H, HD)
        q = (x @ Wq.T + bq).reshape(b, l, h, hd).transpose(0, 2, 1, 3)
        k = (x @ Wk.T + bk).reshape(b, l, h, hd).transpose(0, 2, 1, 3)
        v = (x @ Wv.T + bv).reshape(b, l, h, hd).transpose(0, 2, 1, 3)
        scores = jnp.einsum('bhqd,bhkd->bhqk', q, k) / math.sqrt(hd)
        causal = jnp.tril(jnp.ones((l, l), bool))
        scores = jnp.where(causal, scores, -jnp.inf)
        att = jax.nn.softmax(scores, axis=-1)
        out = jnp.einsum('bhqk,bhkd->bhqd', att, v)
        out = out.transpose(0, 2, 1, 3).reshape(b, l, d)
        return out @ Wo.T + bo

    def _L0_ffn_ref(x, gate_q, gate_absmax, up_q, up_absmax, down_q, down_absmax):
        import jax, jax.numpy as jnp
        import numpy as np
        BLOCK = 64
        NF4_CODE = jnp.array([-1.0, -0.6961928009986877, -0.5250730514526367, -0.39491748809814453, -0.28444138169288635, -0.18477343022823334, -0.09105003625154495, 0.0, 0.07958029955625534, 0.16093020141124725, 0.24611230194568634, 0.33791524171829224, 0.44070982933044434, 0.5626170039176941, 0.7229568362236023, 1.0], dtype=jnp.float32)

        def dequant_nf4(q, absmax, shape):
            w = NF4_CODE[q.reshape(-1)]
            w = w.reshape(-1, BLOCK) * absmax[:, None]
            return w.reshape(shape)
        HD = x.shape[-1]
        M = gate_q.shape[0]
        Wg = dequant_nf4(gate_q, gate_absmax, (M, HD))
        Wu = dequant_nf4(up_q, up_absmax, (M, HD))
        Wd = dequant_nf4(down_q, down_absmax, (HD, M))
        g = jnp.einsum('bsh,mh->bsm', x, Wg)
        u = jnp.einsum('bsh,mh->bsm', x, Wu)
        h = jax.nn.silu(g) * u
        return jnp.einsum('bsm,hm->bsh', h, Wd)
    x = L0_attn_x
    x = _layernorm(x + _L0_attn_ref(x, L0_attn_Wq, L0_attn_bq, L0_attn_Wk, L0_attn_bk, L0_attn_Wv, L0_attn_bv, L0_attn_Wo, L0_attn_bo), axis=-1)
    x = _layernorm(x + _L0_ffn_ref(x, L0_ffn_gate_q, L0_ffn_gate_absmax, L0_ffn_up_q, L0_ffn_up_absmax, L0_ffn_down_q, L0_ffn_down_absmax), axis=-1)
    return x

_drawn_inputs = setup_inputs


def setup_inputs(seed=0):
    import zlib

    import numpy as np

    out = dict(_drawn_inputs(seed))
    spreads = {}
    factors = {'L0_attn_bq': 7.474,
     'L0_attn_bk': 8.0,
     'L0_ffn_gate_absmax': 3.006,
     'L0_ffn_up_absmax': 3.03,
     'L0_ffn_down_absmax': 3.027}
    for name, (base, spread) in spreads.items():
        noise = np.random.default_rng([zlib.crc32(name.encode()), seed]).standard_normal(out[name].shape)
        drawn = base * np.exp(spread * noise) if base else spread * noise
        out[name] = jnp.asarray(drawn.astype(out[name].dtype))
    for name, factor in factors.items():
        out[name] = (out[name] * factor).astype(out[name].dtype)
    return out
```

```python
from contextlib import ExitStack

import numpy as np

import concourse.bass as bass
from concourse import mybir

ALU = mybir.AluOpType
ACT = mybir.ActivationFunctionType
AX_X = mybir.AxisListType.X
F32 = mybir.dt.float32
F32R = mybir.dt.float32r
F16 = mybir.dt.float16
BF16 = mybir.dt.bfloat16

P = 128
B, L, D, H = 8, 256, 512, 32
HD = D // H
M = 1792
KT = D // P
QT = L // P
TILES = B * QT
PAIRS = H // 2
GROUPS = H // 4
CAUSAL = P + L
VW = 3 * HD + 1
VS = VW + 1
PSCALE = 2048.0
BIG = 1.0e30
EPS = 1e-5

MT = M // P
MPAIRS = MT // 2
CHUNK = 4 * P
CHUNKS = TILES // 4
UNITS = 6

LEFT = [(0.30380722880363464, 1.1266505718231201), (0.1301555633544922, 0.12570475041866302),
        (0.09966795146465302, 0.01456246618181467)]
LEFT_LAST = 0.09105003625154495
RIGHT = [(0.08134990185499191, -0.0017695986898615956), (0.0918029397726059, -0.0292965117841959),
         (0.12190717458724976, -0.16882602870464325), (0.2770431637763977, -1.2163453102111816)]
LINES = LEFT + RIGHT
ZERO_CODE = 7.0

FILL = {s: [] for s in range(H)}
for n, task in enumerate([("qk", 0, 2), ("qk", 1, 2), ("qk", 2, 2), ("qk", 3, 2), ("o", 0, 0), ("o", 0, 1),
                          ("qk", 4, 2), ("qk", 5, 2), ("o", 1, 0), ("o", 1, 1), ("qk", 6, 2), ("qk", 7, 2),
                          ("v", 0, 0), ("v", 0, 1), ("v", 1, 0), ("v", 1, 1)]):
    FILL[min(2 * n + 1, 30)].append(task)
FILL[4].append(("aT", 0, 2))
FILL[5].append(("aT", 1, 2))
for g in range(PAIRS):
    FILL[4 + 2 * g if g < PAIRS - 3 else 31].append(("stack", g, 2))


def tasks_of(first, last):
    steps, flat = {}, []
    for s in range(H):
        steps[s] = []
        for kind, n, half in FILL[s]:
            if (kind in ("aT", "o") and first) or (kind in ("qk", "stack", "v") and last):
                continue
            if half != 1:
                flat.append((kind, n))
            steps[s].append((kind, n, half, flat.index((kind, n))))
    return steps, flat


def attention_phase(nc, y, ident, x_t, x_tok, w_t, b_qk, b_v, b_o):
    with ExitStack() as ctx:
        def sb(name, shape, dt):
            return ctx.enter_context(nc.sbuf_tensor(name, shape, dt))

        def sem(name):
            return ctx.enter_context(nc.semaphore(name))

        w_hi = sb("w_hi", [P, 4, KT, D], F32R)
        w_lo = sb("w_lo", [P, 4, KT, D], F32R)
        stack = sb("stack", [P, PAIRS, 2 * L], F32R)
        v_parts = sb("v_parts", [P, 2, QT, H, VW], BF16)
        x_in = sb("x_in", [P, KT, L], F32)
        x_hi = sb("x_hi", [P, KT, L], F32R)
        x_lo = sb("x_lo", [P, KT, L], F32R)
        qk_hi = sb("qk_hi", [P, 2, 2, L], F32R)
        qk_lo = sb("qk_lo", [P, 2, 2, L], F32R)
        sel = sb("sel", [P, 4, 4, P], F32R)
        mask = sb("mask", [P, L], F32)
        masked = sb("masked", [P, 2, CAUSAL], F32)
        low = sb("low", [P, 2, QT], F32)
        probs = sb("probs", [P, 2, CAUSAL], F32)
        pt_hi = sb("pt_hi", [P, 4, CAUSAL], F16)
        pt_lo = sb("pt_lo", [P, 4, CAUSAL], F16)
        att = sb("att", [P, QT, D], F32)
        at_hi = sb("at_hi", [P, QT, D], F32R)
        at_lo = sb("at_lo", [P, QT, D], F32R)
        bqk = sb("bqk", [P, 2 * KT], F32)
        bv = sb("bv", [P, D], F32)
        bo = sb("bo", [P, D], F32)
        v_sum = sb("v_sum", [P, D], F32)
        v_rest = sb("v_rest", [P, D], F32)
        o_sum = sb("o_sum", [P, 8, HD], F32)
        o_inv = sb("o_inv", [P, 8], F32)
        stats = sb("stats", [P, 6], F32)
        moments = sb("moments", [P, 2], F32)
        rs = sb("rs", [P, 4], F32)
        consts = sb("consts", [P, 3], F32)

        ps_s = [ctx.enter_context(nc.psum_tensor(f"ps_s{i}", [P, 512], F32)) for i in range(2)]
        ps_t = [ctx.enter_context(nc.psum_tensor(f"ps_t{i}", [P, 512], F32)) for i in range(2)]
        ps_o = [ctx.enter_context(nc.psum_tensor(f"ps_o{i}", [P, 512], F32)) for i in range(2)]
        ps_x = [ctx.enter_context(nc.psum_tensor(f"ps_x{i}", [P, 512], F32)) for i in range(2)]

        w_loaded = [sem(f"w_loaded{i}") for i in range(4)]
        x_loaded = sem("x_loaded")
        tok_loaded = sem("tok_loaded")
        b_loaded = sem("b_loaded")
        ident_zero, ident_done = sem("ident_zero"), sem("ident_done")
        mask_zero, mask_done = sem("mask_zero"), sem("mask_done")
        sel_zero, sel_done = sem("sel_zero"), sem("sel_done")
        ones_done, bq_done, consts_done = sem("ones_done"), sem("bq_done"), sem("consts_done")
        w_hi_done, w_lo_done = sem("w_hi_done"), sem("w_lo_done")
        x_hi_done, x_lo_done = sem("x_hi_done"), sem("x_lo_done")
        qk_done, qk_hi_done, qk_lo_done = sem("qk_done"), sem("qk_hi_done"), sem("qk_lo_done")
        stack_done, stack_copied = sem("stack_done"), sem("stack_copied")
        v_done, v_summed = sem("v_done"), sem("v_summed")
        v1_done, v_rest_done, v2_done, v3_done = sem("v1_done"), sem("v_rest_done"), sem("v2_done"), sem("v3_done")
        scores_done, masked_done, probs_done = sem("scores_done"), sem("masked_done"), sem("probs_done")
        pt_done, pt_hi_done, pt_lo_done = sem("pt_done"), sem("pt_hi_done"), sem("pt_lo_done")
        pv_done, o_inv_done, o_sum_done, att_done = sem("pv_done"), sem("o_inv_done"), sem("o_sum_done"), sem("att_done")
        at_done, at_hi_done, at_lo_done = sem("at_done"), sem("at_hi_done"), sem("at_lo_done")
        o_done, bo_added, z_done = sem("o_done"), sem("bo_added"), sem("z_done")
        stats_done, moments_done, rs_done, x1_done = sem("stats_done"), sem("moments_done"), sem("rs_done"), sem("x1_done")
        pool_step = sem("pool_step")

        stage = y[:].rearrange("p (w k n) -> p w k n", w=4, k=KT)

        def w_scale(w):
            return -1.0 / 4.0 if w == 0 else 1.0

        def evacuated(kind, n, b):
            return {"qk": (qk_lo_done, 8 * (b + 1) + n + 1), "stack": (stack_copied, 16 * (b + 1) + n + 1),
                    "v": (v_summed, 2 * (b + 1) + n + 1), "aT": (at_lo_done, 2 * (b - 1) + n + 1),
                    "o": (z_done, 2 * (b - 1) + n + 1)}[kind]

        START = [("qk", n) for n in range(4)]
        for f in range(KT):
            START += [("stack", g) for g in range(4 * f, 4 * f + 4)]
            START += [("qk", n) for n in (2 * f + 4, 2 * f + 5) if n < 2 * KT]
        START += [("v", t) for t in range(QT)]

        block = ctx.enter_context(nc.Block())

        @block.sync
        def _(sp):
            sp.dma_start(x_in[:], x_t[0]).then_inc(x_loaded, 16)
            for w in range(4):
                sp.dma_start(stage[:, w], w_t[w]).then_inc(w_loaded[w], 16)
                if w == 0:
                    sp.dma_start(bqk[:], b_qk).then_inc(b_loaded, 16)
                    sp.dma_start(bv[:], b_v.to_broadcast([P, D])).then_inc(b_loaded, 16)
                    sp.dma_start(bo[:], b_o.to_broadcast([P, D])).then_inc(b_loaded, 16)
            sp.wait_ge(x_lo_done, 1)
            sp.dma_start(x_in[:], x_t[1]).then_inc(x_loaded, 16)
            sp.wait_ge(w_lo_done, 4)
            sp.dma_start(y[:].rearrange("p (t n) -> p t n", t=TILES), x_tok).then_inc(tok_loaded, 16)
            with sp.Fori(2, B) as b:
                sp.wait_ge(x_lo_done, b)
                sp.dma_start(x_in[:], x_t[bass.ds(b, 1)].rearrange("a p k n -> p (a k) n")).then_inc(x_loaded, 16)

        @block.gpsimd
        def _(pool):
            nc.gpsimd.memset(sel[:].bitcast(F32), 0.0).then_inc(sel_zero, 1)
            nc.gpsimd.memset(ident[:], 0.0).then_inc(ident_zero, 1)
            nc.gpsimd.memset(mask[:], 0.0).then_inc(mask_zero, 1)
            for n, value in enumerate((EPS, -0.5, 1.5)):
                nc.gpsimd.memset(consts[:, n:n + 1], value).then_inc(consts_done, 1)
            pool.wait_ge(consts_done, 3)
            nc.gpsimd.memset(v_parts[:, :, :, :, 3 * HD:VW], 1.0).then_inc(ones_done, 1)
            pool.wait_ge(sel_zero, 1)
            for kind, copies in ((0, slice(0, 4, 2)), (1, slice(1, 4, 2)), (2, slice(0, 2)), (3, slice(2, 4))):
                for pair in range(4):
                    for c in range(4)[copies]:
                        cols = sel[:, kind, pair].rearrange("p (e c d) -> p e c d", e=2, c=4)[:, :, c, :]
                        nc.gpsimd.affine_select(
                            out=cols, in_=cols.bitcast(F32), compare_op=ALU.not_equal, fill=1.0,
                            base=-32 * pair, pattern=[[-16, 2], [-1, 16]], channel_multiplier=1,
                        ).then_inc(sel_done, 1)
            pool.wait_ge(ident_zero, 1)
            nc.gpsimd.affine_select(out=ident[:], in_=ident[:], compare_op=ALU.not_equal, fill=1.0, base=0,
                                    pattern=[[-1, P]], channel_multiplier=1).then_inc(ident_done, 1)
            pool.wait_ge(mask_zero, 1)
            nc.gpsimd.affine_select(out=mask[:, P:L], in_=mask[:, P:L], compare_op=ALU.is_ge, fill=BIG, base=0,
                                    pattern=[[-1, P]], channel_multiplier=1).then_inc(mask_done, 1)
            pool.wait_ge(b_loaded, 48)

            def v_rest_step(b, par, t):
                if not (isinstance(b, int) and 2 * b + t == 0):
                    pool.wait_ge(v3_done, 2 * b + t)
                pool.wait_ge(v1_done, 2 * b + t + 1)
                nc.gpsimd.tensor_tensor(v_rest[:].rearrange("p (h d) -> p h d", h=H),
                                        v_sum[:].rearrange("p (h d) -> p h d", h=H),
                                        v_parts[:, par, t, :, 0:HD], ALU.subtract).then_inc(v_rest_done, 1)
                pool.wait_ge(v2_done, 2 * b + t + 1)
                nc.gpsimd.tensor_tensor(v_parts[:, par, t, :, 2 * HD:3 * HD],
                                        v_rest[:].rearrange("p (h d) -> p h d", h=H),
                                        v_parts[:, par, t, :, HD:2 * HD], ALU.subtract).then_inc(v3_done, 1)

            def normalise_heads(b, g):
                pool.wait_ge(o_sum_done, 8 * b + g + 1)
                out = att[:, :, 4 * g * HD:4 * (g + 1) * HD].rearrange("p t (h d) -> p t h d", h=4)
                inv = o_inv[:].rearrange("p (t h) -> p t h", t=QT).unsqueeze(3).to_broadcast([P, QT, 4, HD])
                nc.gpsimd.tensor_tensor(out, o_sum[:].rearrange("p (t h) d -> p t h d", t=QT), inv,
                                        ALU.mult).then_inc(att_done, 1)

            def add_bo(b):
                for t in range(QT):
                    cols = y[:, bass.ds((2 * b + t) * D, D)]
                    nc.gpsimd.tensor_tensor(cols, cols, bo[:], ALU.add).then_inc(bo_added, 1)

            def root(b, t):
                rstd_steps(nc, pool, moments, rs, consts, moments_done, 2 * b + t + 1, pool_step, RSTD_STEPS * (2 * b + t),
                           rs_done)

            def batch(b, par, first, last):
                for s in range(H):
                    if s == 0:
                        add_bo(b)
                    if s == 3 and not first:
                        normalise_heads(b - 1, GROUPS - 1)
                    if s >= 7 and s % 4 == 3:
                        normalise_heads(b, (s - 7) // 4)
                    if s == 13 and not first:
                        root(b - 1, 0)
                    if s == 21 and not first:
                        root(b - 1, 1)
                    if s in (28, 31) and not last:
                        v_rest_step(b + 1, 1 - par, (s - 28) // 3)

            pool.wait_ge(tok_loaded, 16)
            for t in range(QT):
                v_rest_step(0, 0, t)
            batch(0, 0, True, False)
            with pool.Fori(0, (B - 2) // 2) as i:
                batch(2 * i + 1, 1, False, False)
                batch(2 * i + 2, 0, False, False)
            batch(B - 1, 1, False, True)
            normalise_heads(B - 1, GROUPS - 1)
            for t in range(QT):
                root(B - 1, t)

        @block.scalar
        def _(act):
            def split_x(b):
                act.wait_ge(x_loaded, 16 * b + 16)
                if not (isinstance(b, int) and b == 0):
                    act.wait_ge(v_done, 2 * b)
                nc.scalar.activation(x_hi[:], x_in[:], ACT.Copy).then_inc(x_hi_done, 1)

            def evacuate(kind, n, bank, b, par):
                if kind == "qk":
                    f, w = n // 2, n % 2
                    act.wait_ge(qk_done, 8 * b + n + 1)
                    if not (isinstance(b, int) and b == 0 and f < 2):
                        act.wait_ge(stack_done, 16 * b + 4 * (f - 2) + 4)
                    nc.scalar.activation(qk_hi[:, f % 2, w], ps_x[bank][:, 0:L], ACT.Identity,
                                         bias=bqk[:, KT * w + f:KT * w + f + 1]).then_inc(qk_hi_done, 1)
                elif kind == "stack":
                    act.wait_ge(stack_done, 16 * b + n + 1)
                    nc.scalar.activation(stack[:, n], ps_x[bank][:], ACT.Copy).then_inc(stack_copied, 1)
                elif kind == "v":
                    act.wait_ge(v_summed, 2 * b + n + 1)
                    nc.scalar.activation(v_parts[:, par, n, :, 0:HD], v_sum[:].rearrange("p (h d) -> p h d", h=H),
                                         ACT.Copy).then_inc(v1_done, 1)
                elif kind == "aT":
                    act.wait_ge(at_done, 2 * b + n + 1)
                    nc.scalar.activation(at_hi[:, n], ps_x[bank][:], ACT.Copy).then_inc(at_hi_done, 1)

            def v2_step(b, par, t):
                act.wait_ge(v_rest_done, 2 * b + t + 1)
                nc.scalar.activation(v_parts[:, par, t, :, HD:2 * HD], v_rest[:].rearrange("p (h d) -> p h d", h=H),
                                     ACT.Copy).then_inc(v2_done, 1)

            def high_halves(b, h):
                head = 32 * b + h
                act.wait_ge(pt_done, head + 1)
                if not (isinstance(head, int) and head < 4):
                    act.wait_ge(pv_done, head - 3)
                nc.scalar.activation(pt_hi[:, h % 4], ps_t[h % 2][:, 0:CAUSAL], ACT.Copy,
                                     scale=PSCALE).then_inc(pt_hi_done, 1)

            def batch(b, par, first, last):
                steps, flat = tasks_of(first, last)
                for s in range(H):
                    act.wait_ge(masked_done, 32 * b + s + 1)
                    if not (first and s < 2):
                        act.wait_ge(pt_done, 32 * b + s - 1)
                    for t, cols in ((0, slice(0, P)), (1, slice(P, CAUSAL))):
                        last_exp = nc.scalar.activation(probs[:, s % 2, cols], masked[:, s % 2, cols], ACT.Exp,
                                                        bias=low[:, s % 2, t:t + 1], scale=-1.0)
                    last_exp.then_inc(probs_done, 1)
                    if s > 0:
                        high_halves(b, s - 1)
                    elif not first:
                        high_halves(b - 1, H - 1)
                    if s == 0 and not last:
                        split_x(b + 1)
                    for kind, n, half_, k in steps[s]:
                        if half_:
                            evacuate(kind, n, k % 2, b - 1 if kind in ("aT", "o") else b + 1,
                                     1 - par)
                    if s in (28, 31) and not last:
                        v2_step(b + 1, 1 - par, (s - 28) // 3)

            for w in range(4):
                act.wait_ge(w_loaded[w], 16)
                nc.scalar.activation(w_hi[:, w], stage[:, w], ACT.Copy, scale=w_scale(w)).then_inc(w_hi_done, 1)
                if w == 0:
                    split_x(0)
                    act.wait_ge(b_loaded, 48)
                    nc.scalar.activation(bqk[:, 0:KT], bqk[:, 0:KT], ACT.Copy, scale=w_scale(0)).then_inc(bq_done, 1)
            act.wait_ge(bq_done, 1)
            act.wait_ge(ones_done, 1)
            for k, (kind, n) in enumerate(START):
                evacuate(kind, n, k % 2, 0, 0)
                if kind == "v":
                    v2_step(0, 0, n)
            batch(0, 0, True, False)
            with act.Fori(0, (B - 2) // 2) as i:
                batch(2 * i + 1, 1, False, False)
                batch(2 * i + 2, 0, False, False)
            batch(B - 1, 1, False, True)
            high_halves(B - 1, H - 1)
            for t in range(QT):
                evacuate("aT", t, t, B - 1, 0)

        @block.vector
        def _(dve):
            heads = dve.alloc_register("heads")
            dve.reg_mov(heads, 0)

            def split_x(b):
                dve.wait_ge(x_hi_done, b + 1)
                nc.vector.tensor_tensor(x_lo[:], x_in[:], x_hi[:].bitcast(F32), ALU.subtract).then_inc(x_lo_done, 1)

            def evacuate(kind, n, bank, b):
                if kind == "qk":
                    f, w = n // 2, n % 2
                    dve.wait_ge(qk_hi_done, 8 * b + n + 1)
                    nc.vector.scalar_tensor_tensor(
                        qk_lo[:, f % 2, w], ps_x[bank][:, 0:L], bqk[:, KT * w + f:KT * w + f + 1],
                        qk_hi[:, f % 2, w].bitcast(F32), ALU.add, ALU.subtract).then_inc(qk_lo_done, 1)
                elif kind == "v":
                    dve.wait_ge(v_done, 2 * b + n + 1)
                    if not (isinstance(b, int) and b == 0 and n == 0):
                        dve.wait_ge(v_rest_done, 2 * b + n)
                    nc.vector.tensor_tensor(v_sum[:], ps_x[bank][:], bv[:], ALU.add).then_inc(v_summed, 1)
                elif kind == "aT":
                    dve.wait_ge(at_hi_done, 2 * b + n + 1)
                    nc.vector.tensor_tensor(at_lo[:, n], ps_x[bank][:], at_hi[:, n].bitcast(F32),
                                            ALU.subtract).then_inc(at_lo_done, 1)
                elif kind == "o":
                    dve.wait_ge(o_done, 2 * b + n + 1)
                    dve.wait_ge(bo_added, 2 * b + n + 1)
                    cols = y[:, bass.ds((2 * b + n) * D, D)]
                    nc.vector.tensor_tensor(cols, ps_x[bank][:], cols, ALU.add).then_inc(z_done, 1)

            def layernorm(b, t, stage_):
                cols = y[:, bass.ds((2 * b + t) * D, D)]
                if stage_ == 0:
                    dve.wait_ge(tok_loaded, 16)
                    dve.wait_ge(z_done, 2 * b + t + 1)
                    nc.vector.bn_stats(stats[:], cols).then_inc(stats_done, 1)
                elif stage_ == 1:
                    dve.wait_ge(tok_loaded, 16)
                    dve.wait_ge(stats_done, 2 * b + t + 1)
                    nc.vector.bn_aggr(moments[:], stats[:]).then_inc(moments_done, 1)
                else:
                    dve.wait_ge(rs_done, 2 * b + t + 1)
                    nc.vector.tensor_scalar(cols, cols, moments[:, 0:1], rs[:, 3:4], ALU.subtract,
                                            ALU.mult).then_inc(x1_done, 1)

            def sum_heads(b, g):
                dve.wait_ge(pv_done, 32 * b + 4 * g + 4)
                if not (isinstance(b, int) and b == 0 and g == 0):
                    dve.wait_ge(att_done, 8 * b + g)
                out = ps_o[g % 2][:, 0:8 * VS].rearrange("p (h c) -> p h c", c=VS)
                nc.vector.reciprocal(o_inv[:].unsqueeze(2), out[:, :, 3 * HD:VW])
                nc.vector.tensor_reduce(o_sum[:], out[:, :, 0:3 * HD].rearrange("p h (c d) -> p h d c", c=3),
                                        axis=AX_X, op=ALU.add).then_inc(o_sum_done, 1)

            def low_halves(b, h):
                dve.wait_ge(pt_hi_done, 32 * b + h + 1)
                nc.vector.scalar_tensor_tensor(pt_lo[:, h % 4], ps_t[h % 2][:, 0:CAUSAL], PSCALE, pt_hi[:, h % 4],
                                               ALU.mult, ALU.subtract).then_inc(pt_lo_done, 1)

            def batch(b, par, first, last):
                steps, flat = tasks_of(first, last)
                for s in range(H):
                    dve.reg_add(heads, heads, 1)
                    dve.wait_ge(mask_done, 1)
                    dve.wait_ge(scores_done, heads)
                    for t, cols, part in ((0, slice(0, P), slice(P, L)), (1, slice(P, CAUSAL), slice(0, L))):
                        last_min = nc.vector.tensor_tensor_reduce(
                            out=masked[:, s % 2, cols], in0=ps_s[s % 2][:, cols], in1=mask[:, part], scale=1.0,
                            scalar=3.0e38, op0=ALU.add, op1=ALU.min, accum_out=low[:, s % 2, t:t + 1])
                    last_min.then_inc(masked_done, 1)
                    if s > 1:
                        low_halves(b, s - 2)
                    elif not first:
                        low_halves(b - 1, H - 2 + s)
                    if s == 0 and not last:
                        split_x(b + 1)
                    if s == 3 and not first:
                        sum_heads(b - 1, GROUPS - 1)
                    if s >= 7 and s % 4 == 3:
                        sum_heads(b, (s - 7) // 4)
                    for kind, n, half_, k in steps[s]:
                        if half_:
                            evacuate(kind, n, k % 2, b - 1 if kind in ("aT", "o") else b + 1)
                    if s in (12, 13, 15) and not first:
                        layernorm(b - 1, 0, {12: 0, 13: 1, 15: 2}[s])
                    if s in (20, 21, 23) and not first:
                        layernorm(b - 1, 1, {20: 0, 21: 1, 23: 2}[s])

            for w in range(4):
                dve.wait_ge(w_hi_done, w + 1)
                nc.vector.scalar_tensor_tensor(
                    w_lo[:, w].rearrange("p k n -> p (k n)"), stage[:, w].rearrange("p k n -> p (k n)"), w_scale(w),
                    w_hi[:, w].rearrange("p k n -> p (k n)").bitcast(F32), ALU.mult, ALU.subtract,
                ).then_inc(w_lo_done, 1)
                if w == 0:
                    split_x(0)
            dve.wait_ge(bq_done, 1)
            for k, (kind, n) in enumerate(START):
                evacuate(kind, n, k % 2, 0)
            batch(0, 0, True, False)
            with dve.Fori(0, (B - 2) // 2) as i:
                batch(2 * i + 1, 1, False, False)
                batch(2 * i + 2, 0, False, False)
            batch(B - 1, 1, False, True)
            low_halves(B - 1, H - 2)
            low_halves(B - 1, H - 1)
            sum_heads(B - 1, GROUPS - 1)
            for t in range(QT):
                evacuate("aT", t, t, B - 1)
            for t in range(QT):
                evacuate("o", t, t, B - 1)
                for stage_ in range(3):
                    layernorm(B - 1, t, stage_)

        @block.tensor
        def _(pe):
            def products(out, parts, first, last):
                todo = [(s, m) for s_hi, s_lo, m_hi, m_lo in parts for s, m in ((s_hi, m_hi), (s_hi, m_lo), (s_lo, m_hi))]
                for n, (s, m) in list(enumerate(todo))[first:last]:
                    done = nc.tensor.matmul(out, s, m, start=n == 0, stop=n == len(todo) - 1)
                return done

            def task(kind, n, half_, bank, b, b_of):
                out = ps_x[bank]
                first, last = {0: (0, 6), 1: (6, 12), 2: (0, 12)}[half_]
                if kind == "qk":
                    f, w = n // 2, n % 2
                    pe.wait_ge(x_lo_done, b_of + 1)
                    cols = slice(f * P, (f + 1) * P)
                    products(out[:, 0:L], [(w_hi[:, w, k, cols], w_lo[:, w, k, cols], x_hi[:, k], x_lo[:, k])
                                           for k in range(KT)], first, last).then_inc(qk_done, 1)
                elif kind == "stack":
                    f, pair = n // 4, n % 4
                    pe.wait_ge(qk_lo_done, 8 * b_of + 2 * f + 2)
                    for w in range(2):
                        half_out = out[:, w * L:(w + 1) * L]
                        nc.tensor.matmul(half_out, sel[:, 2 * w, pair], qk_hi[:, f % 2, w], start=True, stop=False)
                        done = nc.tensor.matmul(half_out, sel[:, 2 * w + 1, pair], qk_lo[:, f % 2, w],
                                                start=False, stop=True)
                    done.then_inc(stack_done, 1)
                elif kind == "v":
                    rows = slice(n * P, (n + 1) * P)
                    done = products(out[:], [(x_hi[:, k, rows], x_lo[:, k, rows], w_hi[:, 2, k], w_lo[:, 2, k])
                                             for k in range(KT)], first, last)
                    if half_:
                        done.then_inc(v_done, 1)
                elif kind == "aT":
                    pe.wait_ge(att_done, 8 * b_of + 8)
                    for f in range(KT):
                        done = nc.tensor.transpose(out[:, f * P:(f + 1) * P], att[:, n, f * P:(f + 1) * P], ident[:])
                    done.then_inc(at_done, 1)
                elif kind == "o":
                    pe.wait_ge(at_lo_done, 2 * b_of + n + 1)
                    done = products(out[:], [(at_hi[:, n, f * P:(f + 1) * P], at_lo[:, n, f * P:(f + 1) * P],
                                              w_hi[:, 3, f], w_lo[:, 3, f]) for f in range(KT)], first, last)
                    if half_:
                        done.then_inc(o_done, 1)

            def transpose_probs(head, ring):
                pe.wait_ge(probs_done, head + 1)
                if not (isinstance(head, int) and head < 2):
                    pe.wait_ge(pt_lo_done, head - 1)
                for c in range(3):
                    done = nc.tensor.transpose(ps_t[ring][:, c * P:(c + 1) * P], probs[:, ring, c * P:(c + 1) * P],
                                               ident[:])
                done.then_inc(pt_done, 1)

            def values(b, par, h):
                g, j = h // 4, h % 4
                pe.wait_ge(pt_lo_done, 32 * b + h + 1)
                if h == 0:
                    pe.wait_ge(v3_done, 2 * b + 2)
                if j == 0 and not (isinstance(b, int) and b == 0 and g < 2):
                    pe.wait_ge(o_sum_done, 8 * b + g - 1)
                for t, blocks in ((0, ((0, 0),)), (1, ((1, 0), (2, 1)))):
                    out = ps_o[g % 2][:, (4 * t + j) * VS:(4 * t + j) * VS + VW]
                    todo = [(pt, c, k) for c, k in blocks for pt in (pt_hi, pt_lo)]
                    for n, (pt, c, k) in enumerate(todo):
                        done = nc.tensor.matmul(out, pt[:, j, c * P:(c + 1) * P], v_parts[:, par, k, h],
                                                start=n == 0, stop=n == len(todo) - 1)
                done.then_inc(pv_done, 1)

            def fill(tasks, flat, b, first):
                for kind, n, half_, k in tasks:
                    if half_ != 1:
                        if k >= 2:
                            pe.wait_ge(*evacuated(*flat[k - 2], b))
                        else:
                            pe.wait_ge(*last_evacuated(b, k, first))
                    task(kind, n, half_, k % 2, b, b - 1 if kind in ("aT", "o") else b + 1)

            def batch(b, par, first, last):
                steps, flat = tasks_of(first, last)
                for s in range(H):
                    g, rows = s // 2, slice(64 * (s % 2), 64 * (s % 2) + 64)
                    if s % 2 == 0:
                        pe.wait_ge(stack_copied, 16 * b + g + 1)
                    if not (first and s < 2):
                        pe.wait_ge(masked_done, 32 * b + s - 1)
                    for t in range(QT):
                        done = nc.tensor.matmul(ps_s[s % 2][:, t * P:t * P + (t + 1) * P],
                                                stack[rows, g, t * P:(t + 1) * P],
                                                stack[rows, g, L:L + (t + 1) * P], start=True, stop=True)
                    done.then_inc(scores_done, 1)
                    fill(steps[s][:2], flat, b, first)
                    if not (first and s == 0):
                        transpose_probs(32 * b + s - 1, (s - 1) % 2)
                    if s > 2:
                        values(b, par, s - 3)
                    elif not first:
                        values(b - 1, 1 - par, H - 3 + s)
                    fill(steps[s][2:], flat, b, first)

            def last_evacuated(b, k, first):
                kind, n = (START if first else tasks_of(False, False)[1])[-2:][k]
                return evacuated(kind, n, b - 1)

            pe.wait_ge(sel_done, 32)
            pe.wait_ge(ident_done, 1)
            pe.wait_ge(w_lo_done, 2)
            for k, (kind, n) in enumerate(START):
                if kind == "v" and n == 0:
                    pe.wait_ge(w_lo_done, 4)
                if k >= 2:
                    pe.wait_ge(*evacuated(*START[k - 2], -1))
                task(kind, n, 2, k % 2, -1, 0)
            batch(0, 0, True, False)
            with pe.Fori(0, (B - 2) // 2) as i:
                batch(2 * i + 1, 1, False, False)
                batch(2 * i + 2, 0, False, False)
            batch(B - 1, 1, False, True)
            transpose_probs(32 * B - 1, 1)
            for h in range(H - 3, H):
                values(B - 1, 1, h)
            for t in range(QT):
                pe.wait_ge(z_done, 2 * (B - 2) + t + 1)
                task("aT", t, 2, t, B, B - 1)
            for t in range(QT):
                pe.wait_ge(at_lo_done, 2 * (B - 1) + t + 1)
                task("o", t, 2, t, B, B - 1)


def rstd_steps(nc, pool, moments, rs, consts, ready, count, steps, steps_before, done):
    pool.wait_ge(ready, count)
    nc.gpsimd.tensor_tensor(rs[:, 0:1], moments[:, 1:2], consts[:, 0:1], ALU.add).then_inc(steps, 1)
    pool.wait_ge(steps, steps_before + 1)
    nc.gpsimd.tensor_tensor(rs[:, 1:2], rs[:, 0:1], consts[:, 1:2], ALU.pow).then_inc(steps, 1)
    pool.wait_ge(steps, steps_before + 2)
    nc.gpsimd.tensor_tensor(rs[:, 2:3], rs[:, 1:2], rs[:, 1:2], ALU.mult).then_inc(steps, 1)
    pool.wait_ge(steps, steps_before + 3)
    nc.gpsimd.tensor_tensor(rs[:, 2:3], rs[:, 2:3], rs[:, 0:1], ALU.mult).then_inc(steps, 1)
    pool.wait_ge(steps, steps_before + 4)
    nc.gpsimd.tensor_tensor(rs[:, 2:3], rs[:, 2:3], consts[:, 1:2], ALU.mult).then_inc(steps, 1)
    pool.wait_ge(steps, steps_before + 5)
    nc.gpsimd.tensor_tensor(rs[:, 2:3], rs[:, 2:3], consts[:, 2:3], ALU.add).then_inc(steps, 1)
    pool.wait_ge(steps, steps_before + 6)
    nc.gpsimd.tensor_tensor(rs[:, 3:4], rs[:, 1:2], rs[:, 2:3], ALU.mult).then_inc(done, 1)


RSTD_STEPS = 6


def ffn_phase(nc, y, ident, gate_q, up_q, down_q, gate_a, up_a, down_a, out):
    with ExitStack() as ctx:
        def sb(name, shape, dt):
            return ctx.enter_context(nc.sbuf_tensor(name, shape, dt))

        def sem(name):
            return ctx.enter_context(nc.semaphore(name))

        xt_hi = sb("xt_hi", [P, KT, TILES * P], F32R)
        xt_lo = sb("xt_lo", [P, KT, TILES * P], F32R)
        wt_hi = sb("wt_hi", [P, 2, 2, 3, D], F32R)
        wt_lo = sb("wt_lo", [P, 2, 2, 3, D], F32R)
        h_hi = sb("h_hi", [P, 2, 2, CHUNK], F32R)
        h_lo = sb("h_lo", [P, 2, 2, CHUNK], F32R)
        silu_g = sb("silu_g", [P, 2, CHUNK], F32)
        hid = sb("hid", [P, 2, CHUNK], F32)
        codes = sb("codes", [P, 2, D], mybir.dt.int32)
        scales = sb("scales", [P, 2, D], F32)
        z = sb("z", [P, 2, D], F32)
        lines = sb("lines", [P, len(LINES), D], F32)
        left = sb("left", [P, D], F32)
        right = sb("right", [P, D], F32)
        w = sb("w", [P, 2, D], F32)
        stats = sb("f_stats", [P, 2, 6], F32)
        moments = sb("f_moments", [P, 2], F32)
        rs = sb("f_rs", [P, 4], F32)
        consts = sb("f_consts", [P, 3], F32)

        ps_g = [ctx.enter_context(nc.psum_tensor(f"ps_g{i}", [P, 512], F32)) for i in range(2)]
        ps_u = [ctx.enter_context(nc.psum_tensor(f"ps_u{i}", [P, 512], F32)) for i in range(2)]
        ps_y = [ctx.enter_context(nc.psum_tensor(f"ps_y{i}", [P, 512], F32)) for i in range(4)]

        loaded = [sem(f"f_loaded{i}") for i in range(2)]
        consts_done = sem("f_consts_done")
        z_done, line_done, deq, w_hi_done, w_lo_done = (
            sem("f_z_done"), sem("line_done"), sem("deq"), sem("f_w_hi_done"), sem("f_w_lo_done"))
        xt_done, xt_hi_done, xt_lo_done = sem("xt_done"), sem("xt_hi_done"), sem("xt_lo_done")
        gate_done, up_done, silu_done = sem("gate_done"), sem("up_done"), sem("silu_done")
        hid_done, h_hi_done, h_lo_done = sem("hid_done"), sem("h_hi_done"), sem("h_lo_done")
        down_done, added = sem("down_done"), sem("added")
        stats_done, moments_done, rs_done, pool_step, norm_done, stored = (
            sem("f_stats_done"), sem("f_moments_done"), sem("f_rs_done"), sem("f_pool_step"), sem("norm_done"),
            sem("stored"))

        DEQ = 8
        L1, R1, L2, R2, L3, R3, CODE, SCALED = range(DEQ)

        def unit(u):
            return u // 3, u % 3

        def weights_by(slot):
            return 54 * slot // 8

        def lines_by(slot):
            done = weights_by(slot)
            return done // 9 * 9 + (8 if done % 9 else 0)

        block = ctx.enter_context(nc.Block())

        @block.sync
        def _(sp):
            def load(pair, u, first):
                tile, matrix = unit(u)
                if not (first and u < 2):
                    sp.wait_ge(z_done, 6 * pair + u - 1)
                    sp.wait_ge(deq, DEQ * (6 * pair + u - 2) + SCALED + 1)
                q = (gate_q, up_q, down_q)[matrix]
                a = (gate_a, up_a, down_a)[matrix]
                j = 2 * pair + tile
                sp.dma_start(codes[:, u % 2], q[bass.ds(j, 1)].rearrange("a p n -> (a p) n")).then_inc(loaded[u % 2], 16)
                for side in range(2):
                    row = a[bass.ds(j, 1), side, :].to_broadcast([64, D])
                    sp.dma_start(scales[64 * side:64 * side + 64, u % 2], row).then_inc(loaded[u % 2], 16)

            for u in range(UNITS):
                load(0, u, True)
            with sp.Fori(1, MPAIRS) as pair:
                for u in range(UNITS):
                    load(pair, u, False)
            for t in range(TILES):
                sp.wait_ge(norm_done, t + 1)
                sp.dma_start(out[t], y[:, t * D:(t + 1) * D]).then_inc(stored, 16)
            sp.wait_ge(stored, 16 * TILES)

        @block.gpsimd
        def _(pool):
            for n, value in enumerate((EPS, -0.5, 1.5)):
                nc.gpsimd.memset(consts[:, n:n + 1], value).then_inc(consts_done, 1)
            pool.wait_ge(consts_done, 3)
            for t in range(TILES):
                if t:
                    pool.wait_ge(norm_done, t)
                rstd_steps(nc, pool, moments, rs, consts, moments_done, t + 1, pool_step, RSTD_STEPS * t, rs_done)

        @block.scalar
        def _(act):
            def dequant(pair, par, k, first):
                u, n = k // 9, k % 9
                tile, matrix = unit(u)
                count = 6 * pair + u
                if n == 0:
                    act.wait_ge(loaded[u % 2], 48 * (3 * pair + u // 2 + 1))
                    if not (first and u < 2):
                        act.wait_ge(deq, DEQ * (count - 2) + L3 + 1)
                    nc.scalar.activation(z[:, u % 2], codes[:, u % 2], ACT.Copy, bias=-ZERO_CODE).then_inc(z_done, 1)
                elif n < 8:
                    if n == 1:
                        act.wait_ge(z_done, count + 1)
                    if not (first and u == 0):
                        reader = (L1, L1, L2, R1, R1, R2, R3)[n - 1]
                        act.wait_ge(deq, DEQ * (count - 1) + reader + 1)
                    slope, at_zero = LINES[n - 1]
                    nc.scalar.activation(lines[:, n - 1], z[:, u % 2], ACT.Copy, scale=slope, bias=at_zero
                                         ).then_inc(line_done, 1)
                else:
                    act.wait_ge(deq, DEQ * count + SCALED + 1)
                    if not (isinstance(pair, int) and pair < 2):
                        if matrix < 2:
                            act.wait_ge(up_done, 8 * (pair - 1))
                        else:
                            act.wait_ge(down_done, 16 * (pair - 1))
                    nc.scalar.activation(wt_hi[:, par, tile, matrix], w[:, u % 2], ACT.Copy).then_inc(w_hi_done, 1)

            def hidden(step, par, tile, first):
                count = 2 * step + tile
                act.wait_ge(gate_done, count + 1)
                if not (first and step == 0):
                    act.wait_ge(hid_done, count - 1)
                nc.scalar.activation(silu_g[:, tile], ps_g[tile][:], ACT.Silu).then_inc(silu_done, 1)

            def high_half(step, par, tile, first):
                count = 2 * step + tile
                act.wait_ge(hid_done, count + 1)
                if not (first and step < 2):
                    act.wait_ge(down_done, 4 * (step - 1))
                nc.scalar.activation(h_hi[:, par, tile], hid[:, tile], ACT.Copy).then_inc(h_hi_done, 1)

            def pair_steps(pair, par, first, last):
                for c in range(CHUNKS):
                    step = 4 * pair + c
                    for tile in range(2):
                        if not last:
                            for k in range(lines_by(2 * c + tile), lines_by(2 * c + tile + 1)):
                                dequant(pair + 1, 1 - par, k, False)
                        hidden(step, c % 2, tile, first)
                        high_half(step, c % 2, tile, first)

            for k in range(54):
                dequant(0, 0, k, True)
            for n in range(KT * CHUNKS):
                act.wait_ge(xt_done, n + 1)
                nc.scalar.activation(xt_hi[:, n % KT, (n // KT) * CHUNK:(n // KT + 1) * CHUNK], ps_y[n % 4][:],
                                     ACT.Copy).then_inc(xt_hi_done, 1)
            pair_steps(0, 0, True, False)
            with act.Fori(0, (MPAIRS - 3) // 2) as i:
                pair_steps(2 * i + 1, 1, False, False)
                pair_steps(2 * i + 2, 0, False, False)
            pair_steps(MPAIRS - 2, 1, False, False)
            pair_steps(MPAIRS - 1, 0, False, True)

        @block.vector
        def _(dve):
            def dequant(pair, par, k, first):
                u, n = k // 9, k % 9
                tile, matrix = unit(u)
                count = 6 * pair + u
                before = DEQ * count
                ready = 7 * count
                if n == L1:
                    dve.wait_ge(line_done, ready + 2)
                    nc.vector.tensor_tensor(left[:], lines[:, 0], lines[:, 1], ALU.min).then_inc(deq, 1)
                elif n == R1:
                    dve.wait_ge(line_done, ready + 5)
                    nc.vector.scalar_tensor_tensor(right[:], lines[:, 3], 0.0, lines[:, 4], ALU.max,
                                                   ALU.max).then_inc(deq, 1)
                elif n == L2:
                    dve.wait_ge(deq, before + L1 + 1)
                    nc.vector.tensor_tensor(left[:], left[:], lines[:, 2], ALU.min).then_inc(deq, 1)
                elif n == R2:
                    dve.wait_ge(line_done, ready + 6)
                    dve.wait_ge(deq, before + R1 + 1)
                    nc.vector.tensor_tensor(right[:], right[:], lines[:, 5], ALU.max).then_inc(deq, 1)
                elif n == L3:
                    dve.wait_ge(deq, before + L2 + 1)
                    nc.vector.scalar_tensor_tensor(left[:], z[:, u % 2], LEFT_LAST, left[:], ALU.mult,
                                                   ALU.min).then_inc(deq, 1)
                elif n == R3:
                    dve.wait_ge(line_done, ready + 7)
                    dve.wait_ge(deq, before + R2 + 1)
                    nc.vector.tensor_tensor(right[:], right[:], lines[:, 6], ALU.max).then_inc(deq, 1)
                elif n == CODE:
                    dve.wait_ge(deq, before + R3 + 1)
                    if not (first and u < 2):
                        dve.wait_ge(w_lo_done, count - 1)
                    nc.vector.scalar_tensor_tensor(w[:, u % 2], left[:], 0.0, right[:], ALU.min,
                                                   ALU.add).then_inc(deq, 1)
                elif n == SCALED:
                    dve.wait_ge(deq, before + CODE + 1)
                    dve.wait_ge(loaded[u % 2], 48 * (3 * pair + u // 2 + 1))
                    nc.vector.tensor_tensor(w[:, u % 2], w[:, u % 2], scales[:, u % 2], ALU.mult).then_inc(deq, 1)
                else:
                    dve.wait_ge(w_hi_done, count + 1)
                    nc.vector.tensor_tensor(wt_lo[:, par, tile, matrix], w[:, u % 2],
                                            wt_hi[:, par, tile, matrix].bitcast(F32), ALU.subtract
                                            ).then_inc(w_lo_done, 1)

            def hidden(step, par, tile, first):
                count = 2 * step + tile
                dve.wait_ge(up_done, count + 1)
                dve.wait_ge(silu_done, count + 1)
                if not (first and step == 0):
                    dve.wait_ge(h_lo_done, count - 1)
                nc.vector.tensor_tensor(hid[:, tile], ps_u[tile][:], silu_g[:, tile], ALU.mult).then_inc(hid_done, 1)

            def low_half(step, par, tile):
                dve.wait_ge(h_hi_done, 2 * step + tile + 1)
                nc.vector.tensor_tensor(h_lo[:, par, tile], hid[:, tile], h_hi[:, par, tile].bitcast(F32),
                                        ALU.subtract).then_inc(h_lo_done, 1)

            def add(step, c):
                for r in range(4):
                    cols = y[:, (4 * c + r) * D:(4 * c + r + 1) * D]
                    dve.wait_ge(down_done, 4 * step + r + 1)
                    nc.vector.tensor_tensor(cols, ps_y[r][:], cols, ALU.add).then_inc(added, 1)

            def normalise(c):
                for t in range(4 * c, 4 * c + 4):
                    cols = y[:, t * D:(t + 1) * D]
                    dve.wait_ge(added, 4 * (4 * (MPAIRS - 1)) + t + 1)
                    nc.vector.bn_stats(stats[:, t % 2], cols).then_inc(stats_done, 1)
                    dve.wait_ge(stats_done, t + 1)
                    nc.vector.bn_aggr(moments[:], stats[:, t % 2]).then_inc(moments_done, 1)
                    dve.wait_ge(rs_done, t + 1)
                    nc.vector.tensor_scalar(cols, cols, moments[:, 0:1], rs[:, 3:4], ALU.subtract,
                                            ALU.mult).then_inc(norm_done, 1)

            def pair_steps(pair, par, first, last):
                for c in range(CHUNKS):
                    step = 4 * pair + c
                    if not (first and c < 2):
                        add(step - 2, (c - 2) % 4)
                    if last and c >= 2:
                        normalise(c - 2)
                    for tile in range(2):
                        if not last:
                            for k in range(weights_by(2 * c + tile), weights_by(2 * c + tile + 1)):
                                dequant(pair + 1, 1 - par, k, False)
                        hidden(step, c % 2, tile, first)
                        low_half(step, c % 2, tile)

            for k in range(54):
                dequant(0, 0, k, True)
            for n in range(KT * CHUNKS):
                dve.wait_ge(xt_hi_done, n + 1)
                cols = slice((n // KT) * CHUNK, (n // KT + 1) * CHUNK)
                nc.vector.tensor_tensor(xt_lo[:, n % KT, cols], ps_y[n % 4][:], xt_hi[:, n % KT, cols].bitcast(F32),
                                        ALU.subtract).then_inc(xt_lo_done, 1)
            pair_steps(0, 0, True, False)
            with dve.Fori(0, (MPAIRS - 3) // 2) as i:
                pair_steps(2 * i + 1, 1, False, False)
                pair_steps(2 * i + 2, 0, False, False)
            pair_steps(MPAIRS - 2, 1, False, False)
            pair_steps(MPAIRS - 1, 0, False, True)
            for c in range(2, 4):
                add(4 * (MPAIRS - 1) + c, c)
                normalise(c)

        @block.tensor
        def _(pe):
            def gate_up(step, par, tile, c, first):
                count = 2 * step + tile
                if not (first and step == 0):
                    pe.wait_ge(hid_done, count - 1)
                cols = slice(c * CHUNK, (c + 1) * CHUNK)
                for matrix, bank, done_sem in ((0, ps_g[tile], gate_done), (1, ps_u[tile], up_done)):
                    n = 0
                    for k in range(KT):
                        hi = wt_hi[:, par, tile, matrix, k * P:(k + 1) * P]
                        lo = wt_lo[:, par, tile, matrix, k * P:(k + 1) * P]
                        for s, m in ((hi, xt_hi), (hi, xt_lo), (lo, xt_hi)):
                            done = nc.tensor.matmul(bank[:], s, m[:, k, cols], start=n == 0, stop=n == 3 * KT - 1)
                            n += 1
                    done.then_inc(done_sem, 1)

            def down(step, par, w_par, first):
                pe.wait_ge(h_lo_done, 2 * step + 2)
                for r in range(4):
                    if first:
                        pe.wait_ge(xt_lo_done, KT * CHUNKS)
                    else:
                        pe.wait_ge(added, 4 * (step - 1) + r + 1)
                    rows = slice(r * P, (r + 1) * P)
                    n = 0
                    for tile in range(2):
                        w_hi, w_lo = wt_hi[:, w_par, tile, 2], wt_lo[:, w_par, tile, 2]
                        for s, m in ((h_hi, w_hi), (h_hi, w_lo), (h_lo, w_hi)):
                            done = nc.tensor.matmul(ps_y[r][:], s[:, par, tile, rows], m, start=n == 0, stop=n == 5)
                            n += 1
                    done.then_inc(down_done, 1)

            def pair_steps(pair, par, first, last):
                pe.wait_ge(w_lo_done, 6 * pair + 6)
                for c in range(CHUNKS):
                    step = 4 * pair + c
                    for tile in range(2):
                        gate_up(step, par, tile, c, first)
                    if not (first and c == 0):
                        down(step - 1, (c - 1) % 2, par if c else 1 - par, first and c == 1)

            for n in range(KT * CHUNKS):
                f, c = n % KT, n // KT
                if n >= 4:
                    pe.wait_ge(xt_lo_done, n - 3)
                for r in range(4):
                    t = 4 * c + r
                    done = nc.tensor.transpose(ps_y[n % 4][:, r * P:(r + 1) * P],
                                               y[:, t * D + f * P:t * D + (f + 1) * P], ident[:])
                done.then_inc(xt_done, 1)
            pe.wait_ge(xt_lo_done, KT * CHUNKS)
            pair_steps(0, 0, True, False)
            with pe.Fori(0, (MPAIRS - 3) // 2) as i:
                pair_steps(2 * i + 1, 1, False, False)
                pair_steps(2 * i + 2, 0, False, False)
            pair_steps(MPAIRS - 2, 1, False, False)
            pair_steps(MPAIRS - 1, 0, False, True)
            down(4 * MPAIRS - 1, 1, 0, False)


def build(nc, x_t, x_tok, w_t, b_qk, b_v, b_o, gate_q, up_q, down_q, gate_a, up_a, down_a, out):
    with nc.sbuf_tensor("y", [P, TILES * D], F32) as y, nc.sbuf_tensor("ident", [P, P], F32) as ident:
        attention_phase(nc, y, ident, x_t, x_tok, w_t, b_qk, b_v, b_o)
        ffn_phase(nc, y, ident, gate_q, up_q, down_q, gate_a, up_a, down_a, out)


def kernel(L0_attn_x, L0_attn_Wq, L0_attn_bq, L0_attn_Wk, L0_attn_bk, L0_attn_Wv, L0_attn_bv, L0_attn_Wo, L0_attn_bo,
           L0_ffn_gate_q, L0_ffn_gate_absmax, L0_ffn_up_q, L0_ffn_up_absmax, L0_ffn_down_q, L0_ffn_down_absmax):
    import concourse.bacc as bacc
    from concourse.bass_utils import run_bass_kernel_spmd

    def features(w):
        return np.asarray(w).T.reshape(KT, P, D).transpose(1, 0, 2)

    def hidden_q(q):
        return np.asarray(q).reshape(MT, P, KT, P).transpose(0, 3, 2, 1).reshape(MT, P, D)

    def hidden_a(a):
        return np.asarray(a).reshape(MT, P, KT, 2).transpose(0, 3, 2, 1).reshape(MT, 2, D)

    x = np.asarray(L0_attn_x).reshape(TILES * P, D)
    arrays = {
        "x_t": x.reshape(B, L, KT, P).transpose(0, 3, 2, 1),
        "x_tok": x.reshape(TILES, P, D).transpose(1, 0, 2),
        "w_t": np.stack([features(w) for w in (L0_attn_Wq, L0_attn_Wk, L0_attn_Wv, L0_attn_Wo)]),
        "b_qk": np.concatenate([np.asarray(b).reshape(KT, P).T for b in (L0_attn_bq, L0_attn_bk)], axis=1),
        "b_v": np.asarray(L0_attn_bv).reshape(1, D),
        "b_o": np.asarray(L0_attn_bo).reshape(1, D),
        "gate_q": hidden_q(L0_ffn_gate_q),
        "up_q": hidden_q(L0_ffn_up_q),
        "down_q": np.asarray(L0_ffn_down_q).T.reshape(MT, P, D),
        "gate_a": hidden_a(L0_ffn_gate_absmax),
        "up_a": hidden_a(L0_ffn_up_absmax),
        "down_a": np.asarray(L0_ffn_down_absmax).reshape(D, MT, 2).transpose(1, 2, 0),
    }
    arrays = {name: np.ascontiguousarray(a) for name, a in arrays.items()}
    nc = bacc.Bacc("TRN2", target_bir_lowering=False, num_devices=1)
    args = [nc.dram_tensor(name, a.shape, mybir.dt.from_np(a.dtype), kind="ExternalInput").ap()
            for name, a in arrays.items()]
    out = nc.dram_tensor("out", (TILES, P, D), F32, kind="ExternalOutput").ap()
    build(nc, *args, out)
    r = run_bass_kernel_spmd(nc, [arrays], core_ids=[0])
    return r.results[0]["out"].reshape(B, L, D)
```

```python
from contextlib import ExitStack

import numpy as np

import concourse.bass as bass
from concourse import mybir

ALU = mybir.AluOpType
ACT = mybir.ActivationFunctionType
AX_X = mybir.AxisListType.X
F32 = mybir.dt.float32
F32R = mybir.dt.float32r
F16 = mybir.dt.float16
BF16 = mybir.dt.bfloat16

P = 128
B, L, D, H = 8, 256, 512, 32
HD = D // H
M = 1792
KT = D // P
QT = L // P
TILES = B * QT
PAIRS = H // 2
GROUPS = H // 4
CAUSAL = P + L
VW = 3 * HD + 1
VS = VW + 1
PSCALE = 2048.0
BIG = 1.0e30
EPS = 1e-5

MT = M // P
MPAIRS = MT // 2
CHUNK = 4 * P
CHUNKS = TILES // 4
UNITS = 6

LEFT = [(0.30380722880363464, 1.1266505718231201), (0.1301555633544922, 0.12570475041866302),
        (0.09966795146465302, 0.01456246618181467)]
LEFT_LAST = 0.09105003625154495
RIGHT = [(0.08134990185499191, -0.0017695986898615956), (0.0918029397726059, -0.0292965117841959),
         (0.12190717458724976, -0.16882602870464325), (0.2770431637763977, -1.2163453102111816)]
LINES = LEFT + RIGHT
ZERO_CODE = 7.0

HALVES = ([("qk", n, 2) for n in range(4)] + [("o", 0, 0), ("o", 0, 1), ("qk", 4, 2), ("qk", 5, 2), ("o", 1, 0),
          ("o", 1, 1), ("qk", 6, 2), ("qk", 7, 2)] + [("v", t, half) for t in range(QT) for half in range(2)])
FILL = {s: [] for s in range(H)}
for n, task in enumerate(HALVES):
    FILL[min(2 * n + 1, 30)].append(task + (0,))
for t in range(QT):
    FILL[5 + 2 * t].append(("aT", t, 2, 1))
for g in range(PAIRS):
    FILL[min(4 + 2 * g, 31)].append(("stack", g, 2, g != 14))


def tasks_of(first, last):
    steps, before = {}, [None, None]
    for s in range(H):
        steps[s] = []
        for kind, n, half, bank in FILL[s]:
            if (kind in ("aT", "o") and first) or (kind in ("qk", "stack", "v") and last):
                continue
            steps[s].append((kind, n, half, int(bank), before[bank]))
            before[bank] = (kind, n)
    return steps, before


def attention_phase(nc, y, ident, x_t, x_tok, w_t, b_qk, b_v, b_o):
    with ExitStack() as ctx:
        def sb(name, shape, dt):
            return ctx.enter_context(nc.sbuf_tensor(name, shape, dt))

        def sem(name):
            return ctx.enter_context(nc.semaphore(name))

        w_hi = sb("w_hi", [P, 4, KT, D], F32R)
        w_lo = sb("w_lo", [P, 4, KT, D], F32R)
        stack = sb("stack", [P, PAIRS, 2 * L], F32R)
        v_parts = sb("v_parts", [P, 2, QT, H, VW], BF16)
        x_in = sb("x_in", [P, KT, L], F32)
        x_hi = sb("x_hi", [P, KT, L], F32R)
        x_lo = sb("x_lo", [P, KT, L], F32R)
        qk_hi = sb("qk_hi", [P, 2, 2, L], F32R)
        qk_lo = sb("qk_lo", [P, 2, 2, L], F32R)
        sel = sb("sel", [P, 4, 4, P], F32R)
        mask = sb("mask", [P, L], F32)
        masked = sb("masked", [P, 2, CAUSAL], F32)
        low = sb("low", [P, 2, QT], F32)
        probs = sb("probs", [P, 2, CAUSAL], F32)
        pt_hi = sb("pt_hi", [P, 4, CAUSAL], F16)
        pt_lo = sb("pt_lo", [P, 4, CAUSAL], F16)
        att = sb("att", [P, QT, D], F32)
        at_hi = sb("at_hi", [P, QT, D], F32R)
        at_lo = sb("at_lo", [P, QT, D], F32R)
        bqk = sb("bqk", [P, 2 * KT], F32)
        bv = sb("bv", [P, D], F32)
        bo = sb("bo", [P, D], F32)
        v_sum = sb("v_sum", [P, D], F32)
        v_rest = sb("v_rest", [P, D], F32)
        o_sum = sb("o_sum", [P, 8, HD], F32)
        o_inv = sb("o_inv", [P, 8], F32)
        stats = sb("stats", [P, 6], F32)
        moments = sb("moments", [P, 2], F32)
        rs = sb("rs", [P, 4], F32)
        consts = sb("consts", [P, 3], F32)

        ps_s = [ctx.enter_context(nc.psum_tensor(f"ps_s{i}", [P, 512], F32)) for i in range(2)]
        ps_t = [ctx.enter_context(nc.psum_tensor(f"ps_t{i}", [P, 512], F32)) for i in range(2)]
        ps_o = [ctx.enter_context(nc.psum_tensor(f"ps_o{i}", [P, 512], F32)) for i in range(2)]
        ps_x = [ctx.enter_context(nc.psum_tensor(f"ps_x{i}", [P, 512], F32)) for i in range(2)]

        w_loaded = [sem(f"w_loaded{i}") for i in range(4)]
        x_loaded = sem("x_loaded")
        tok_loaded = sem("tok_loaded")
        b_loaded = sem("b_loaded")
        ident_zero, ident_done = sem("ident_zero"), sem("ident_done")
        mask_zero, mask_done = sem("mask_zero"), sem("mask_done")
        sel_zero, sel_done = sem("sel_zero"), sem("sel_done")
        ones_done, bq_done, consts_done = sem("ones_done"), sem("bq_done"), sem("consts_done")
        w_hi_done, w_lo_done = sem("w_hi_done"), sem("w_lo_done")
        x_hi_done, x_lo_done = sem("x_hi_done"), sem("x_lo_done")
        qk_done, qk_hi_done, qk_lo_done = sem("qk_done"), sem("qk_hi_done"), sem("qk_lo_done")
        stack_done, stack_copied = sem("stack_done"), sem("stack_copied")
        v_done, v_summed = sem("v_done"), sem("v_summed")
        v1_done, v_rest_done, v2_done, v3_done = sem("v1_done"), sem("v_rest_done"), sem("v2_done"), sem("v3_done")
        scores_done, masked_done, probs_done = sem("scores_done"), sem("masked_done"), sem("probs_done")
        pt_done, pt_hi_done, pt_lo_done = sem("pt_done"), sem("pt_hi_done"), sem("pt_lo_done")
        pv_done, o_inv_done, o_sum_done, att_done = sem("pv_done"), sem("o_inv_done"), sem("o_sum_done"), sem("att_done")
        at_done, at_hi_done, at_lo_done = sem("at_done"), sem("at_hi_done"), sem("at_lo_done")
        o_done, bo_added, z_done = sem("o_done"), sem("bo_added"), sem("z_done")
        stats_done, moments_done, rs_done, x1_done = sem("stats_done"), sem("moments_done"), sem("rs_done"), sem("x1_done")
        pool_step = sem("pool_step")

        stage = y[:].rearrange("p (w k n) -> p w k n", w=4, k=KT)

        def w_scale(w):
            return -1.0 / 4.0 if w == 0 else 1.0

        def evacuated(kind, n, b):
            return {"qk": (qk_lo_done, 8 * (b + 1) + n + 1), "stack": (stack_copied, 16 * (b + 1) + n + 1),
                    "v": (v_summed, 2 * (b + 1) + n + 1), "aT": (at_lo_done, 2 * (b - 1) + n + 1),
                    "o": (z_done, 2 * (b - 1) + n + 1)}[kind]

        START = [("qk", n) for n in range(4)]
        for f in range(KT):
            START += [("stack", g) for g in range(4 * f, 4 * f + 4)]
            START += [("qk", n) for n in (2 * f + 4, 2 * f + 5) if n < 2 * KT]
        START += [("v", t) for t in range(QT)]

        block = ctx.enter_context(nc.Block())

        @block.sync
        def _(sp):
            sp.dma_start(x_in[:], x_t[0]).then_inc(x_loaded, 16)
            for w in range(4):
                sp.dma_start(stage[:, w], w_t[w]).then_inc(w_loaded[w], 16)
                if w == 0:
                    sp.dma_start(bqk[:], b_qk).then_inc(b_loaded, 16)
                    sp.dma_start(bv[:], b_v.to_broadcast([P, D])).then_inc(b_loaded, 16)
                    sp.dma_start(bo[:], b_o.to_broadcast([P, D])).then_inc(b_loaded, 16)
            sp.wait_ge(x_lo_done, 1)
            sp.dma_start(x_in[:], x_t[1]).then_inc(x_loaded, 16)
            sp.wait_ge(w_lo_done, 4)
            sp.dma_start(y[:].rearrange("p (t n) -> p t n", t=TILES), x_tok).then_inc(tok_loaded, 16)
            with sp.Fori(2, B) as b:
                sp.wait_ge(x_lo_done, b)
                sp.dma_start(x_in[:], x_t[bass.ds(b, 1)].rearrange("a p k n -> p (a k) n")).then_inc(x_loaded, 16)

        @block.gpsimd
        def _(pool):
            nc.gpsimd.memset(sel[:].bitcast(F32), 0.0).then_inc(sel_zero, 1)
            nc.gpsimd.memset(ident[:], 0.0).then_inc(ident_zero, 1)
            nc.gpsimd.memset(mask[:], 0.0).then_inc(mask_zero, 1)
            for n, value in enumerate((EPS, -0.5, 1.5)):
                nc.gpsimd.memset(consts[:, n:n + 1], value).then_inc(consts_done, 1)
            pool.wait_ge(consts_done, 3)
            nc.gpsimd.memset(v_parts[:, :, :, :, 3 * HD:VW], 1.0).then_inc(ones_done, 1)
            pool.wait_ge(sel_zero, 1)
            for kind, copies in ((0, slice(0, 4, 2)), (1, slice(1, 4, 2)), (2, slice(0, 2)), (3, slice(2, 4))):
                for pair in range(4):
                    for c in range(4)[copies]:
                        cols = sel[:, kind, pair].rearrange("p (e c d) -> p e c d", e=2, c=4)[:, :, c, :]
                        nc.gpsimd.affine_select(
                            out=cols, in_=cols.bitcast(F32), compare_op=ALU.not_equal, fill=1.0,
                            base=-32 * pair, pattern=[[-16, 2], [-1, 16]], channel_multiplier=1,
                        ).then_inc(sel_done, 1)
            pool.wait_ge(ident_zero, 1)
            nc.gpsimd.affine_select(out=ident[:], in_=ident[:], compare_op=ALU.not_equal, fill=1.0, base=0,
                                    pattern=[[-1, P]], channel_multiplier=1).then_inc(ident_done, 1)
            pool.wait_ge(mask_zero, 1)
            nc.gpsimd.affine_select(out=mask[:, P:L], in_=mask[:, P:L], compare_op=ALU.is_ge, fill=BIG, base=0,
                                    pattern=[[-1, P]], channel_multiplier=1).then_inc(mask_done, 1)
            pool.wait_ge(b_loaded, 48)

            def v_rest_step(b, par, t):
                if not (isinstance(b, int) and 2 * b + t == 0):
                    pool.wait_ge(v3_done, 2 * b + t)
                pool.wait_ge(v1_done, 2 * b + t + 1)
                nc.gpsimd.tensor_tensor(v_rest[:].rearrange("p (h d) -> p h d", h=H),
                                        v_sum[:].rearrange("p (h d) -> p h d", h=H),
                                        v_parts[:, par, t, :, 0:HD], ALU.subtract).then_inc(v_rest_done, 1)
                pool.wait_ge(v2_done, 2 * b + t + 1)
                nc.gpsimd.tensor_tensor(v_parts[:, par, t, :, 2 * HD:3 * HD],
                                        v_rest[:].rearrange("p (h d) -> p h d", h=H),
                                        v_parts[:, par, t, :, HD:2 * HD], ALU.subtract).then_inc(v3_done, 1)

            def normalise_heads(b, g):
                pool.wait_ge(o_sum_done, 8 * b + g + 1)
                if g == 0 and not (isinstance(b, int) and b == 0):
                    pool.wait_ge(at_done, 2 * b)
                out = att[:, :, 4 * g * HD:4 * (g + 1) * HD].rearrange("p t (h d) -> p t h d", h=4)
                inv = o_inv[:].rearrange("p (t h) -> p t h", t=QT).unsqueeze(3).to_broadcast([P, QT, 4, HD])
                nc.gpsimd.tensor_tensor(out, o_sum[:].rearrange("p (t h) d -> p t h d", t=QT), inv,
                                        ALU.mult).then_inc(att_done, 1)

            def add_bo(b):
                for t in range(QT):
                    cols = y[:, bass.ds((2 * b + t) * D, D)]
                    nc.gpsimd.tensor_tensor(cols, cols, bo[:], ALU.add).then_inc(bo_added, 1)

            def root(b, t):
                rstd_steps(nc, pool, moments, rs, consts, moments_done, 2 * b + t + 1, pool_step, RSTD_STEPS * (2 * b + t),
                           rs_done)

            def batch(b, par, first, last):
                for s in range(H):
                    if s == 0:
                        add_bo(b)
                    if s % 4 == 0 and s >= 8:
                        normalise_heads(b, s // 4 - 2)
                    elif s % 4 == 0 and not first:
                        normalise_heads(b - 1, GROUPS - 2 + s // 4)
                    if s == 13 and not first:
                        root(b - 1, 0)
                    if s == 21 and not first:
                        root(b - 1, 1)
                    if s in (28, 31) and not last:
                        v_rest_step(b + 1, 1 - par, (s - 28) // 3)

            pool.wait_ge(tok_loaded, 16)
            for t in range(QT):
                v_rest_step(0, 0, t)
            batch(0, 0, True, False)
            with pool.Fori(0, (B - 2) // 2) as i:
                batch(2 * i + 1, 1, False, False)
                batch(2 * i + 2, 0, False, False)
            batch(B - 1, 1, False, True)
            normalise_heads(B - 1, GROUPS - 2)
            normalise_heads(B - 1, GROUPS - 1)
            for t in range(QT):
                root(B - 1, t)

        @block.scalar
        def _(act):
            def split_x(b):
                act.wait_ge(x_loaded, 16 * b + 16)
                if not (isinstance(b, int) and b == 0):
                    act.wait_ge(v_done, 2 * b)
                nc.scalar.activation(x_hi[:], x_in[:], ACT.Copy).then_inc(x_hi_done, 1)

            def evacuate(kind, n, bank, b, par):
                if kind == "qk":
                    f, w = n // 2, n % 2
                    act.wait_ge(qk_done, 8 * b + n + 1)
                    if not (isinstance(b, int) and b == 0 and f < 2):
                        act.wait_ge(stack_done, 16 * b + 4 * (f - 2) + 4)
                    nc.scalar.activation(qk_hi[:, f % 2, w], ps_x[bank][:, 0:L], ACT.Identity,
                                         bias=bqk[:, KT * w + f:KT * w + f + 1]).then_inc(qk_hi_done, 1)
                elif kind == "stack":
                    act.wait_ge(stack_done, 16 * b + n + 1)
                    nc.scalar.activation(stack[:, n], ps_x[bank][:], ACT.Copy).then_inc(stack_copied, 1)
                elif kind == "v":
                    act.wait_ge(v_summed, 2 * b + n + 1)
                    nc.scalar.activation(v_parts[:, par, n, :, 0:HD], v_sum[:].rearrange("p (h d) -> p h d", h=H),
                                         ACT.Copy).then_inc(v1_done, 1)
                elif kind == "aT":
                    act.wait_ge(at_done, 2 * b + n + 1)
                    nc.scalar.activation(at_hi[:, n], ps_x[bank][:], ACT.Copy).then_inc(at_hi_done, 1)

            def v2_step(b, par, t):
                act.wait_ge(v_rest_done, 2 * b + t + 1)
                nc.scalar.activation(v_parts[:, par, t, :, HD:2 * HD], v_rest[:].rearrange("p (h d) -> p h d", h=H),
                                     ACT.Copy).then_inc(v2_done, 1)

            def high_halves(b, h):
                head = 32 * b + h
                act.wait_ge(pt_done, head + 1)
                if not (isinstance(head, int) and head < 4):
                    act.wait_ge(pv_done, head - 3)
                nc.scalar.activation(pt_hi[:, h % 4], ps_t[h % 2][:, 0:CAUSAL], ACT.Copy,
                                     scale=PSCALE).then_inc(pt_hi_done, 1)

            def batch(b, par, first, last):
                steps, _ = tasks_of(first, last)
                for s in range(H):
                    if s == 0 and not last:
                        split_x(b + 1)
                    if s > 1:
                        high_halves(b, s - 2)
                    elif not first:
                        high_halves(b - 1, H - 2 + s)
                    act.wait_ge(masked_done, 32 * b + s + 1)
                    if not (first and s < 2):
                        act.wait_ge(pt_done, 32 * b + s - 1)
                    for t, cols in ((0, slice(0, P)), (1, slice(P, CAUSAL))):
                        last_exp = nc.scalar.activation(probs[:, s % 2, cols], masked[:, s % 2, cols], ACT.Exp,
                                                        bias=low[:, s % 2, t:t + 1], scale=-1.0)
                    last_exp.then_inc(probs_done, 1)
                    for kind, n, half_, bank, _ in steps[s]:
                        if half_:
                            evacuate(kind, n, bank, b - 1 if kind in ("aT", "o") else b + 1,
                                     1 - par)
                    if s in (28, 31) and not last:
                        v2_step(b + 1, 1 - par, (s - 28) // 3)

            for w in range(4):
                act.wait_ge(w_loaded[w], 16)
                nc.scalar.activation(w_hi[:, w], stage[:, w], ACT.Copy, scale=w_scale(w)).then_inc(w_hi_done, 1)
                if w == 0:
                    split_x(0)
                    act.wait_ge(b_loaded, 48)
                    nc.scalar.activation(bqk[:, 0:KT], bqk[:, 0:KT], ACT.Copy, scale=w_scale(0)).then_inc(bq_done, 1)
            act.wait_ge(bq_done, 1)
            act.wait_ge(ones_done, 1)
            for k, (kind, n) in enumerate(START):
                evacuate(kind, n, k % 2, 0, 0)
                if kind == "v":
                    v2_step(0, 0, n)
            batch(0, 0, True, False)
            with act.Fori(0, (B - 2) // 2) as i:
                batch(2 * i + 1, 1, False, False)
                batch(2 * i + 2, 0, False, False)
            batch(B - 1, 1, False, True)
            high_halves(B - 1, H - 2)
            high_halves(B - 1, H - 1)
            for t in range(QT):
                evacuate("aT", t, t, B - 1, 0)

        @block.vector
        def _(dve):
            heads = dve.alloc_register("heads")
            dve.reg_mov(heads, 0)

            def split_x(b):
                dve.wait_ge(x_hi_done, b + 1)
                nc.vector.tensor_tensor(x_lo[:], x_in[:], x_hi[:].bitcast(F32), ALU.subtract).then_inc(x_lo_done, 1)

            def evacuate(kind, n, bank, b):
                if kind == "qk":
                    f, w = n // 2, n % 2
                    dve.wait_ge(qk_hi_done, 8 * b + n + 1)
                    nc.vector.scalar_tensor_tensor(
                        qk_lo[:, f % 2, w], ps_x[bank][:, 0:L], bqk[:, KT * w + f:KT * w + f + 1],
                        qk_hi[:, f % 2, w].bitcast(F32), ALU.add, ALU.subtract).then_inc(qk_lo_done, 1)
                elif kind == "v":
                    dve.wait_ge(v_done, 2 * b + n + 1)
                    if not (isinstance(b, int) and b == 0 and n == 0):
                        dve.wait_ge(v_rest_done, 2 * b + n)
                    nc.vector.tensor_tensor(v_sum[:], ps_x[bank][:], bv[:], ALU.add).then_inc(v_summed, 1)
                elif kind == "aT":
                    dve.wait_ge(at_hi_done, 2 * b + n + 1)
                    nc.vector.tensor_tensor(at_lo[:, n], ps_x[bank][:], at_hi[:, n].bitcast(F32),
                                            ALU.subtract).then_inc(at_lo_done, 1)
                elif kind == "o":
                    dve.wait_ge(o_done, 2 * b + n + 1)
                    dve.wait_ge(bo_added, 2 * b + n + 1)
                    cols = y[:, bass.ds((2 * b + n) * D, D)]
                    nc.vector.tensor_tensor(cols, ps_x[bank][:], cols, ALU.add).then_inc(z_done, 1)

            def layernorm(b, t, stage_):
                cols = y[:, bass.ds((2 * b + t) * D, D)]
                if stage_ == 0:
                    dve.wait_ge(tok_loaded, 16)
                    dve.wait_ge(z_done, 2 * b + t + 1)
                    nc.vector.bn_stats(stats[:], cols).then_inc(stats_done, 1)
                elif stage_ == 1:
                    dve.wait_ge(tok_loaded, 16)
                    dve.wait_ge(stats_done, 2 * b + t + 1)
                    nc.vector.bn_aggr(moments[:], stats[:]).then_inc(moments_done, 1)
                else:
                    dve.wait_ge(rs_done, 2 * b + t + 1)
                    nc.vector.tensor_scalar(cols, cols, moments[:, 0:1], rs[:, 3:4], ALU.subtract,
                                            ALU.mult).then_inc(x1_done, 1)

            def sum_heads(b, g):
                dve.wait_ge(pv_done, 32 * b + 4 * g + 4)
                if not (isinstance(b, int) and b == 0 and g == 0):
                    dve.wait_ge(att_done, 8 * b + g)
                out = ps_o[g % 2][:, 0:8 * VS].rearrange("p (h c) -> p h c", c=VS)
                nc.vector.reciprocal(o_inv[:].unsqueeze(2), out[:, :, 3 * HD:VW])
                nc.vector.tensor_reduce(o_sum[:], out[:, :, 0:3 * HD].rearrange("p h (c d) -> p h d c", c=3),
                                        axis=AX_X, op=ALU.add).then_inc(o_sum_done, 1)

            def low_halves(b, h):
                dve.wait_ge(pt_hi_done, 32 * b + h + 1)
                nc.vector.scalar_tensor_tensor(pt_lo[:, h % 4], ps_t[h % 2][:, 0:CAUSAL], PSCALE, pt_hi[:, h % 4],
                                               ALU.mult, ALU.subtract).then_inc(pt_lo_done, 1)

            def batch(b, par, first, last):
                steps, _ = tasks_of(first, last)
                for s in range(H):
                    if s == 0 and not last:
                        split_x(b + 1)
                    dve.reg_add(heads, heads, 1)
                    dve.wait_ge(mask_done, 1)
                    dve.wait_ge(scores_done, heads)
                    for t, cols, part in ((0, slice(0, P), slice(P, L)), (1, slice(P, CAUSAL), slice(0, L))):
                        last_min = nc.vector.tensor_tensor_reduce(
                            out=masked[:, s % 2, cols], in0=ps_s[s % 2][:, cols], in1=mask[:, part], scale=1.0,
                            scalar=3.0e38, op0=ALU.add, op1=ALU.min, accum_out=low[:, s % 2, t:t + 1])
                    last_min.then_inc(masked_done, 1)
                    if s > 1:
                        low_halves(b, s - 2)
                    elif not first:
                        low_halves(b - 1, H - 2 + s)
                    if s % 4 == 0 and s >= 8:
                        sum_heads(b, s // 4 - 2)
                    elif s % 4 == 0 and not first:
                        sum_heads(b - 1, GROUPS - 2 + s // 4)
                    for kind, n, half_, bank, _ in steps[s]:
                        if half_:
                            evacuate(kind, n, bank, b - 1 if kind in ("aT", "o") else b + 1)
                    if s in (12, 13, 15) and not first:
                        layernorm(b - 1, 0, {12: 0, 13: 1, 15: 2}[s])
                    if s in (20, 21, 23) and not first:
                        layernorm(b - 1, 1, {20: 0, 21: 1, 23: 2}[s])

            for w in range(4):
                dve.wait_ge(w_hi_done, w + 1)
                nc.vector.scalar_tensor_tensor(
                    w_lo[:, w].rearrange("p k n -> p (k n)"), stage[:, w].rearrange("p k n -> p (k n)"), w_scale(w),
                    w_hi[:, w].rearrange("p k n -> p (k n)").bitcast(F32), ALU.mult, ALU.subtract,
                ).then_inc(w_lo_done, 1)
                if w == 0:
                    split_x(0)
            dve.wait_ge(bq_done, 1)
            for k, (kind, n) in enumerate(START):
                evacuate(kind, n, k % 2, 0)
            batch(0, 0, True, False)
            with dve.Fori(0, (B - 2) // 2) as i:
                batch(2 * i + 1, 1, False, False)
                batch(2 * i + 2, 0, False, False)
            batch(B - 1, 1, False, True)
            low_halves(B - 1, H - 2)
            low_halves(B - 1, H - 1)
            sum_heads(B - 1, GROUPS - 2)
            sum_heads(B - 1, GROUPS - 1)
            for t in range(QT):
                evacuate("aT", t, t, B - 1)
            for t in range(QT):
                evacuate("o", t, t, B - 1)
                for stage_ in range(3):
                    layernorm(B - 1, t, stage_)

        @block.tensor
        def _(pe):
            def products(out, parts, first, last):
                todo = [(s, m) for s_hi, s_lo, m_hi, m_lo in parts for s, m in ((s_hi, m_hi), (s_hi, m_lo), (s_lo, m_hi))]
                for n, (s, m) in list(enumerate(todo))[first:last]:
                    done = nc.tensor.matmul(out, s, m, start=n == 0, stop=n == len(todo) - 1)
                return done

            def task(kind, n, half_, bank, b, b_of):
                out = ps_x[bank]
                first, last = {0: (0, 6), 1: (6, 12), 2: (0, 12)}[half_]
                if kind == "qk":
                    f, w = n // 2, n % 2
                    pe.wait_ge(x_lo_done, b_of + 1)
                    cols = slice(f * P, (f + 1) * P)
                    products(out[:, 0:L], [(w_hi[:, w, k, cols], w_lo[:, w, k, cols], x_hi[:, k], x_lo[:, k])
                                           for k in range(KT)], first, last).then_inc(qk_done, 1)
                elif kind == "stack":
                    f, pair = n // 4, n % 4
                    pe.wait_ge(qk_lo_done, 8 * b_of + 2 * f + 2)
                    for w in range(2):
                        half_out = out[:, w * L:(w + 1) * L]
                        nc.tensor.matmul(half_out, sel[:, 2 * w, pair], qk_hi[:, f % 2, w], start=True, stop=False)
                        done = nc.tensor.matmul(half_out, sel[:, 2 * w + 1, pair], qk_lo[:, f % 2, w],
                                                start=False, stop=True)
                    done.then_inc(stack_done, 1)
                elif kind == "v":
                    rows = slice(n * P, (n + 1) * P)
                    done = products(out[:], [(x_hi[:, k, rows], x_lo[:, k, rows], w_hi[:, 2, k], w_lo[:, 2, k])
                                             for k in range(KT)], first, last)
                    if half_:
                        done.then_inc(v_done, 1)
                elif kind == "aT":
                    pe.wait_ge(att_done, 8 * b_of + 8)
                    for f in range(KT):
                        done = nc.tensor.transpose(out[:, f * P:(f + 1) * P], att[:, n, f * P:(f + 1) * P], ident[:])
                    done.then_inc(at_done, 1)
                elif kind == "o":
                    pe.wait_ge(at_lo_done, 2 * b_of + n + 1)
                    done = products(out[:], [(at_hi[:, n, f * P:(f + 1) * P], at_lo[:, n, f * P:(f + 1) * P],
                                              w_hi[:, 3, f], w_lo[:, 3, f]) for f in range(KT)], first, last)
                    if half_:
                        done.then_inc(o_done, 1)

            def transpose_probs(head, ring):
                pe.wait_ge(probs_done, head + 1)
                if not (isinstance(head, int) and head < 2):
                    pe.wait_ge(pt_lo_done, head - 1)
                for c in range(3):
                    done = nc.tensor.transpose(ps_t[ring][:, c * P:(c + 1) * P], probs[:, ring, c * P:(c + 1) * P],
                                               ident[:])
                done.then_inc(pt_done, 1)

            def values(b, par, h):
                g, j = h // 4, h % 4
                pe.wait_ge(pt_lo_done, 32 * b + h + 1)
                if h == 0:
                    pe.wait_ge(v3_done, 2 * b + 2)
                if j == 0 and not (isinstance(b, int) and b == 0 and g < 2):
                    pe.wait_ge(o_sum_done, 8 * b + g - 1)
                for t, blocks in ((0, ((0, 0),)), (1, ((1, 0), (2, 1)))):
                    out = ps_o[g % 2][:, (4 * t + j) * VS:(4 * t + j) * VS + VW]
                    todo = [(pt, c, k) for c, k in blocks for pt in (pt_hi, pt_lo)]
                    for n, (pt, c, k) in enumerate(todo):
                        done = nc.tensor.matmul(out, pt[:, j, c * P:(c + 1) * P], v_parts[:, par, k, h],
                                                start=n == 0, stop=n == len(todo) - 1)
                done.then_inc(pv_done, 1)

            def fill(tasks, b, first):
                for kind, n, half_, bank, before in tasks:
                    if half_ != 1:
                        if before:
                            pe.wait_ge(*evacuated(*before, b))
                        else:
                            pe.wait_ge(*last_evacuated(b, bank, first))
                    task(kind, n, half_, bank, b, b - 1 if kind in ("aT", "o") else b + 1)

            def batch(b, par, first, last):
                steps, _ = tasks_of(first, last)
                for s in range(H):
                    g, rows = s // 2, slice(64 * (s % 2), 64 * (s % 2) + 64)
                    if not (first and s < 2):
                        transpose_probs(32 * b + s - 2, s % 2)
                    if s % 2 == 0:
                        pe.wait_ge(stack_copied, 16 * b + g + 1)
                    if not (first and s < 2):
                        pe.wait_ge(masked_done, 32 * b + s - 1)
                    for t in (1, 0):
                        done = nc.tensor.matmul(ps_s[s % 2][:, t * P:t * P + (t + 1) * P],
                                                stack[rows, g, t * P:(t + 1) * P],
                                                stack[rows, g, L:L + (t + 1) * P], start=True, stop=True)
                    done.then_inc(scores_done, 1)
                    if s > 3:
                        values(b, par, s - 4)
                    elif not first:
                        values(b - 1, 1 - par, H - 4 + s)
                    fill(steps[s], b, first)

            def last_evacuated(b, bank, first):
                kind, n = START[-2:][bank] if first else tasks_of(False, False)[1][bank]
                return evacuated(kind, n, b - 1)

            pe.wait_ge(sel_done, 32)
            pe.wait_ge(ident_done, 1)
            pe.wait_ge(w_lo_done, 2)
            for k, (kind, n) in enumerate(START):
                if kind == "v" and n == 0:
                    pe.wait_ge(w_lo_done, 4)
                if k >= 2:
                    pe.wait_ge(*evacuated(*START[k - 2], -1))
                task(kind, n, 2, k % 2, -1, 0)
            batch(0, 0, True, False)
            with pe.Fori(0, (B - 2) // 2) as i:
                batch(2 * i + 1, 1, False, False)
                batch(2 * i + 2, 0, False, False)
            batch(B - 1, 1, False, True)
            transpose_probs(32 * B - 2, 0)
            transpose_probs(32 * B - 1, 1)
            for h in range(H - 4, H):
                values(B - 1, 1, h)
            for t in range(QT):
                pe.wait_ge(z_done, 2 * (B - 2) + t + 1)
                task("aT", t, 2, t, B, B - 1)
            for t in range(QT):
                pe.wait_ge(at_lo_done, 2 * (B - 1) + t + 1)
                task("o", t, 2, t, B, B - 1)


def rstd_steps(nc, pool, moments, rs, consts, ready, count, steps, steps_before, done):
    pool.wait_ge(ready, count)
    nc.gpsimd.tensor_tensor(rs[:, 0:1], moments[:, 1:2], consts[:, 0:1], ALU.add).then_inc(steps, 1)
    pool.wait_ge(steps, steps_before + 1)
    nc.gpsimd.tensor_tensor(rs[:, 1:2], rs[:, 0:1], consts[:, 1:2], ALU.pow).then_inc(steps, 1)
    pool.wait_ge(steps, steps_before + 2)
    nc.gpsimd.tensor_tensor(rs[:, 2:3], rs[:, 1:2], rs[:, 1:2], ALU.mult).then_inc(steps, 1)
    pool.wait_ge(steps, steps_before + 3)
    nc.gpsimd.tensor_tensor(rs[:, 2:3], rs[:, 2:3], rs[:, 0:1], ALU.mult).then_inc(steps, 1)
    pool.wait_ge(steps, steps_before + 4)
    nc.gpsimd.tensor_tensor(rs[:, 2:3], rs[:, 2:3], consts[:, 1:2], ALU.mult).then_inc(steps, 1)
    pool.wait_ge(steps, steps_before + 5)
    nc.gpsimd.tensor_tensor(rs[:, 2:3], rs[:, 2:3], consts[:, 2:3], ALU.add).then_inc(steps, 1)
    pool.wait_ge(steps, steps_before + 6)
    nc.gpsimd.tensor_tensor(rs[:, 3:4], rs[:, 1:2], rs[:, 2:3], ALU.mult).then_inc(done, 1)


RSTD_STEPS = 6


def ffn_phase(nc, y, ident, gate_q, up_q, down_q, gate_a, up_a, down_a, out):
    with ExitStack() as ctx:
        def sb(name, shape, dt):
            return ctx.enter_context(nc.sbuf_tensor(name, shape, dt))

        def sem(name):
            return ctx.enter_context(nc.semaphore(name))

        xt_hi = sb("xt_hi", [P, KT, TILES * P], F32R)
        xt_lo = sb("xt_lo", [P, KT, TILES * P], F32R)
        wt_hi = sb("wt_hi", [P, 2, 2, 3, D], F32R)
        wt_lo = sb("wt_lo", [P, 2, 2, 3, D], F32R)
        h_hi = sb("h_hi", [P, 2, 2, CHUNK], F32R)
        h_lo = sb("h_lo", [P, 2, 2, CHUNK], F32R)
        silu_g = sb("silu_g", [P, 2, CHUNK], F32)
        hid = sb("hid", [P, 2, CHUNK], F32)
        codes = sb("codes", [P, 2, D], mybir.dt.int32)
        scales = sb("scales", [P, 2, D], F32)
        z = sb("z", [P, 2, D], F32)
        lines = sb("lines", [P, len(LINES), D], F32)
        left = sb("left", [P, D], F32)
        right = sb("right", [P, D], F32)
        w = sb("w", [P, 2, D], F32)
        stats = sb("f_stats", [P, 4, 6], F32)
        moments = sb("f_moments", [P, 4, 2], F32)
        rs = sb("f_rs", [P, 4, 4], F32)
        consts = sb("f_consts", [P, 3], F32)

        ps_g = [ctx.enter_context(nc.psum_tensor(f"ps_g{i}", [P, 512], F32)) for i in range(2)]
        ps_u = [ctx.enter_context(nc.psum_tensor(f"ps_u{i}", [P, 512], F32)) for i in range(2)]
        ps_y = [ctx.enter_context(nc.psum_tensor(f"ps_y{i}", [P, 512], F32)) for i in range(4)]

        loaded = [sem(f"f_loaded{i}") for i in range(2)]
        consts_done = sem("f_consts_done")
        z_done, line_done, deq, w_hi_done, w_lo_done = (
            sem("f_z_done"), sem("line_done"), sem("deq"), sem("f_w_hi_done"), sem("f_w_lo_done"))
        scaled = sem("scaled")
        xt_done, xt_hi_done, xt_lo_done = sem("xt_done"), sem("xt_hi_done"), sem("xt_lo_done")
        gate_done, up_done, silu_done = sem("gate_done"), sem("up_done"), sem("silu_done")
        hid_done, h_hi_done, h_lo_done = sem("hid_done"), sem("h_hi_done"), sem("h_lo_done")
        down_done, added = sem("down_done"), sem("added")
        stats_done, moments_done, rs_done, pool_step, norm_done, stored = (
            sem("f_stats_done"), sem("f_moments_done"), sem("f_rs_done"), sem("f_pool_step"), sem("norm_done"),
            sem("stored"))

        L1, R1, L2, R2, L3, R3, CODE = range(7)
        DEQ = 7
        ACT_STEPS = []
        for u in range(UNITS):
            ACT_STEPS += [("z", u, 0)] + [("line", u, n) for n in range(6)]
            ACT_STEPS += [("high", u - 1, 0)] if u else []
            ACT_STEPS += [("line", u, 6)]

        def unit(u):
            return (u // 2, u % 2) if u < 4 else (u - 4, 2)

        SLOTS = 3 * CHUNKS

        def codes_by(slot):
            return DEQ * UNITS * slot // SLOTS

        def lines_by(slot):
            last = codes_by(min(slot + 1, SLOTS)) - 1
            line = (1, 4, 4, 5, 5, 6, 6)[last % DEQ]
            return ACT_STEPS.index(("line", last // DEQ, line)) + 1 if slot else 0

        block = ctx.enter_context(nc.Block())

        @block.sync
        def _(sp):
            def load(pair, u, first):
                tile, matrix = unit(u)
                if not (first and u < 2):
                    sp.wait_ge(z_done, 6 * pair + u - 1)
                    sp.wait_ge(scaled, 6 * pair + u - 1)
                q = (gate_q, up_q, down_q)[matrix]
                a = (gate_a, up_a, down_a)[matrix]
                j = 2 * pair + tile
                sp.dma_start(codes[:, u % 2], q[bass.ds(j, 1)].rearrange("a p n -> (a p) n")).then_inc(loaded[u % 2], 16)
                for side in range(2):
                    row = a[bass.ds(j, 1), side, :].to_broadcast([64, D])
                    sp.dma_start(scales[64 * side:64 * side + 64, u % 2], row).then_inc(loaded[u % 2], 16)

            for u in range(UNITS):
                load(0, u, True)
            with sp.Fori(1, MPAIRS) as pair:
                for u in range(UNITS):
                    load(pair, u, False)
            for t in range(TILES):
                sp.wait_ge(norm_done, t + 1)
                sp.dma_start(out[t], y[:, t * D:(t + 1) * D]).then_inc(stored, 16)
            sp.wait_ge(stored, 16 * TILES)

        @block.gpsimd
        def _(pool):
            for n, value in enumerate((EPS, -0.5, 1.5)):
                nc.gpsimd.memset(consts[:, n:n + 1], value).then_inc(consts_done, 1)
            pool.wait_ge(consts_done, 3)

            def weight_low(pair, par, u):
                tile, matrix = unit(u)
                pool.wait_ge(w_hi_done, 6 * pair + u + 1)
                nc.gpsimd.tensor_tensor(wt_lo[:, par, tile, matrix], w[:, u % 2],
                                        wt_hi[:, par, tile, matrix].bitcast(F32), ALU.subtract).then_inc(w_lo_done, 1)

            def weights(pair, par):
                for u in range(UNITS):
                    pool.wait_ge(deq, DEQ * (6 * pair + u) + CODE + 1)
                    pool.wait_ge(loaded[u % 2], 48 * (3 * pair + u // 2 + 1))
                    nc.gpsimd.tensor_tensor(w[:, u % 2], w[:, u % 2], scales[:, u % 2], ALU.mult).then_inc(scaled, 1)
                    if u:
                        weight_low(pair, par, u - 1)
                weight_low(pair, par, UNITS - 1)

            weights(0, 0)
            with pool.Fori(0, (MPAIRS - 1) // 2) as i:
                weights(2 * i + 1, 1)
                weights(2 * i + 2, 0)
            for t in range(TILES):
                if t >= 4:
                    pool.wait_ge(norm_done, t - 3)
                rstd_steps(nc, pool, moments[:, t % 4], rs[:, t % 4], consts, moments_done, t + 1, pool_step,
                           RSTD_STEPS * t, rs_done)

        @block.scalar
        def _(act):
            def dequant(pair, par, k, first):
                kind, u, n = ACT_STEPS[k]
                count = 6 * pair + u
                if kind == "z":
                    act.wait_ge(loaded[u % 2], 48 * (3 * pair + u // 2 + 1))
                    if not (first and u < 2):
                        act.wait_ge(deq, DEQ * (count - 2) + L3 + 1)
                    nc.scalar.activation(z[:, u % 2], codes[:, u % 2], ACT.Copy, bias=-ZERO_CODE).then_inc(z_done, 1)
                elif kind == "line":
                    if n == 0:
                        act.wait_ge(z_done, count + 1)
                    if not (first and u == 0):
                        reader = (L1, L1, L2, R1, R1, R2, R3)[n]
                        act.wait_ge(deq, DEQ * (count - 1) + reader + 1)
                    slope, at_zero = LINES[n]
                    nc.scalar.activation(lines[:, n], z[:, u % 2], ACT.Copy, scale=slope, bias=at_zero
                                         ).then_inc(line_done, 1)
                else:
                    weight_high(pair, par, u)

            def weight_high(pair, par, u):
                tile, matrix = unit(u)
                act.wait_ge(scaled, 6 * pair + u + 1)
                if not (isinstance(pair, int) and pair < 2):
                    if matrix < 2:
                        act.wait_ge(up_done, 8 * (pair - 1))
                    else:
                        act.wait_ge(down_done, 16 * (pair - 1))
                nc.scalar.activation(wt_hi[:, par, tile, matrix], w[:, u % 2], ACT.Copy).then_inc(w_hi_done, 1)

            def hidden(step, par, tile, first):
                count = 2 * step + tile
                act.wait_ge(gate_done, count + 1)
                if not (first and step == 0):
                    act.wait_ge(hid_done, count - 1)
                nc.scalar.activation(silu_g[:, tile], ps_g[tile][:], ACT.Silu).then_inc(silu_done, 1)

            def high_half(step, par, tile, first):
                count = 2 * step + tile
                act.wait_ge(hid_done, count + 1)
                if not (first and step < 2):
                    act.wait_ge(down_done, 4 * (step - 1))
                nc.scalar.activation(h_hi[:, par, tile], hid[:, tile], ACT.Copy).then_inc(h_hi_done, 1)

            def pair_steps(pair, par, first, last):
                def weights(slot):
                    if not last:
                        for k in range(lines_by(slot), lines_by(slot + 1)):
                            dequant(pair + 1, 1 - par, k, False)

                for c in range(CHUNKS):
                    step = 4 * pair + c
                    weights(3 * c)
                    hidden(step, c % 2, 0, first)
                    weights(3 * c + 1)
                    high_half(step, c % 2, 0, first)
                    hidden(step, c % 2, 1, first)
                    weights(3 * c + 2)
                    high_half(step, c % 2, 1, first)
                if not last:
                    weight_high(pair + 1, 1 - par, UNITS - 1)

            for k in range(len(ACT_STEPS)):
                dequant(0, 0, k, True)
            weight_high(0, 0, UNITS - 1)
            for n in range(KT * CHUNKS):
                act.wait_ge(xt_done, n + 1)
                nc.scalar.activation(xt_hi[:, n % KT, (n // KT) * CHUNK:(n // KT + 1) * CHUNK], ps_y[n % 4][:],
                                     ACT.Copy).then_inc(xt_hi_done, 1)
            pair_steps(0, 0, True, False)
            with act.Fori(0, (MPAIRS - 3) // 2) as i:
                pair_steps(2 * i + 1, 1, False, False)
                pair_steps(2 * i + 2, 0, False, False)
            pair_steps(MPAIRS - 2, 1, False, False)
            pair_steps(MPAIRS - 1, 0, False, True)

        @block.vector
        def _(dve):
            def dequant(pair, k, first):
                u, n = k // DEQ, k % DEQ
                count = 6 * pair + u
                before = DEQ * count
                ready = 7 * count
                if n == L1:
                    dve.wait_ge(line_done, ready + 2)
                    if not (first and u == 0):
                        dve.wait_ge(deq, before)
                    nc.vector.tensor_tensor(left[:], lines[:, 0], lines[:, 1], ALU.min).then_inc(deq, 1)
                elif n == R1:
                    dve.wait_ge(line_done, ready + 5)
                    nc.vector.scalar_tensor_tensor(right[:], lines[:, 3], 0.0, lines[:, 4], ALU.max,
                                                   ALU.max).then_inc(deq, 1)
                elif n == L2:
                    dve.wait_ge(deq, before + L1 + 1)
                    nc.vector.tensor_tensor(left[:], left[:], lines[:, 2], ALU.min).then_inc(deq, 1)
                elif n == R2:
                    dve.wait_ge(line_done, ready + 6)
                    dve.wait_ge(deq, before + R1 + 1)
                    nc.vector.tensor_tensor(right[:], right[:], lines[:, 5], ALU.max).then_inc(deq, 1)
                elif n == L3:
                    dve.wait_ge(deq, before + L2 + 1)
                    nc.vector.scalar_tensor_tensor(left[:], z[:, u % 2], LEFT_LAST, left[:], ALU.mult,
                                                   ALU.min).then_inc(deq, 1)
                elif n == R3:
                    dve.wait_ge(line_done, ready + 7)
                    dve.wait_ge(deq, before + R2 + 1)
                    nc.vector.tensor_tensor(right[:], right[:], lines[:, 6], ALU.max).then_inc(deq, 1)
                else:
                    dve.wait_ge(deq, before + R3 + 1)
                    if not (first and u < 2):
                        dve.wait_ge(w_lo_done, count - 1)
                    nc.vector.scalar_tensor_tensor(w[:, u % 2], left[:], 0.0, right[:], ALU.min,
                                                   ALU.add).then_inc(deq, 1)

            def hidden(step, par, tile, first):
                count = 2 * step + tile
                dve.wait_ge(up_done, count + 1)
                dve.wait_ge(silu_done, count + 1)
                if not (first and step == 0):
                    dve.wait_ge(h_lo_done, count - 1)
                nc.vector.tensor_tensor(hid[:, tile], ps_u[tile][:], silu_g[:, tile], ALU.mult).then_inc(hid_done, 1)

            def low_half(step, par, tile):
                dve.wait_ge(h_hi_done, 2 * step + tile + 1)
                nc.vector.tensor_tensor(h_lo[:, par, tile], hid[:, tile], h_hi[:, par, tile].bitcast(F32),
                                        ALU.subtract).then_inc(h_lo_done, 1)

            def add(step, c, r):
                cols = y[:, (4 * c + r) * D:(4 * c + r + 1) * D]
                dve.wait_ge(down_done, 4 * step + r + 1)
                nc.vector.tensor_tensor(cols, ps_y[r][:], cols, ALU.add).then_inc(added, 1)

            def measure(t):
                dve.wait_ge(added, 4 * (4 * (MPAIRS - 1)) + t + 1)
                nc.vector.bn_stats(stats[:, t % 4], y[:, t * D:(t + 1) * D]).then_inc(stats_done, 1)
                dve.wait_ge(stats_done, t + 1)
                if t >= 4:
                    dve.wait_ge(norm_done, t - 3)
                nc.vector.bn_aggr(moments[:, t % 4], stats[:, t % 4]).then_inc(moments_done, 1)

            def normalise(t):
                cols = y[:, t * D:(t + 1) * D]
                dve.wait_ge(rs_done, t + 1)
                nc.vector.tensor_scalar(cols, cols, moments[:, t % 4, 0:1], rs[:, t % 4, 3:4], ALU.subtract,
                                        ALU.mult).then_inc(norm_done, 1)

            def pair_steps(pair, par, first, last):
                def weights(slot):
                    if not last:
                        for k in range(codes_by(slot), codes_by(slot + 1)):
                            dequant(pair + 1, k, False)

                for c in range(CHUNKS):
                    step = 4 * pair + c
                    if not (first and c < 2):
                        for r in range(4):
                            add(step - 2, (c - 2) % 4, r)
                    weights(3 * c)
                    hidden(step, c % 2, 0, first)
                    if last and c >= 2:
                        for t in range(4 * (c - 2), 4 * (c - 1)):
                            measure(t)
                    weights(3 * c + 1)
                    low_half(step, c % 2, 0)
                    hidden(step, c % 2, 1, first)
                    weights(3 * c + 2)
                    low_half(step, c % 2, 1)
                    if last and c >= 2:
                        for t in range(4 * (c - 2), 4 * (c - 1)):
                            normalise(t)

            for k in range(DEQ * UNITS):
                dequant(0, k, True)
            for n in range(KT * CHUNKS):
                dve.wait_ge(xt_hi_done, n + 1)
                cols = slice((n // KT) * CHUNK, (n // KT + 1) * CHUNK)
                nc.vector.tensor_tensor(xt_lo[:, n % KT, cols], ps_y[n % 4][:], xt_hi[:, n % KT, cols].bitcast(F32),
                                        ALU.subtract).then_inc(xt_lo_done, 1)
            pair_steps(0, 0, True, False)
            with dve.Fori(0, (MPAIRS - 3) // 2) as i:
                pair_steps(2 * i + 1, 1, False, False)
                pair_steps(2 * i + 2, 0, False, False)
            pair_steps(MPAIRS - 2, 1, False, False)
            pair_steps(MPAIRS - 1, 0, False, True)
            for c in range(2, 4):
                for r in range(4):
                    t = 4 * c + r
                    add(4 * (MPAIRS - 1) + c, c, r)
                    measure(t)
                    if r:
                        normalise(t - 1)
                normalise(t)

        @block.tensor
        def _(pe):
            def gate_up(step, par, tile, c, first):
                count = 2 * step + tile
                if not (first and step == 0):
                    pe.wait_ge(hid_done, count - 1)
                cols = slice(c * CHUNK, (c + 1) * CHUNK)
                for matrix, bank, done_sem in ((0, ps_g[tile], gate_done), (1, ps_u[tile], up_done)):
                    n = 0
                    for k in range(KT):
                        hi = wt_hi[:, par, tile, matrix, k * P:(k + 1) * P]
                        lo = wt_lo[:, par, tile, matrix, k * P:(k + 1) * P]
                        for s, m in ((hi, xt_hi), (hi, xt_lo), (lo, xt_hi)):
                            done = nc.tensor.matmul(bank[:], s, m[:, k, cols], start=n == 0, stop=n == 3 * KT - 1)
                            n += 1
                    done.then_inc(done_sem, 1)

            def down(step, par, w_par, first):
                pe.wait_ge(h_lo_done, 2 * step + 2)
                for r in range(4):
                    for tile in range(2):
                        done = down_part(step, par, w_par, first, r, tile)
                    done.then_inc(down_done, 1)

            def down_part(step, par, w_par, first, r, tile):
                if tile == 0:
                    if first:
                        pe.wait_ge(xt_lo_done, KT * CHUNKS)
                    else:
                        pe.wait_ge(added, 4 * (step - 1) + r + 1)
                w_hi, w_lo = wt_hi[:, w_par, tile, 2], wt_lo[:, w_par, tile, 2]
                for n, (s, m) in enumerate(((h_hi, w_hi), (h_hi, w_lo), (h_lo, w_hi))):
                    done = nc.tensor.matmul(ps_y[r][:], s[:, par, tile, r * P:(r + 1) * P], m,
                                            start=tile == 0 and n == 0, stop=tile == 1 and n == 2)
                return done

            def pair_steps(pair, par, first, last):
                for c in range(CHUNKS):
                    step = 4 * pair + c
                    for tile in range(2):
                        if c == 0:
                            pe.wait_ge(w_lo_done, 6 * pair + 2 * tile + 2)
                        gate_up(step, par, tile, c, first)
                    if c == 1:
                        pe.wait_ge(w_lo_done, 6 * pair + 6)
                    if not (first and c == 0):
                        down(step - 1, (c - 1) % 2, par if c else 1 - par, first and c == 1)

            for n in range(KT * CHUNKS):
                f, c = n % KT, n // KT
                if n >= 4:
                    pe.wait_ge(xt_lo_done, n - 3)
                for r in range(4):
                    t = 4 * c + r
                    done = nc.tensor.transpose(ps_y[n % 4][:, r * P:(r + 1) * P],
                                               y[:, t * D + f * P:t * D + (f + 1) * P], ident[:])
                done.then_inc(xt_done, 1)
            pe.wait_ge(xt_lo_done, KT * CHUNKS)
            pair_steps(0, 0, True, False)
            with pe.Fori(0, (MPAIRS - 3) // 2) as i:
                pair_steps(2 * i + 1, 1, False, False)
                pair_steps(2 * i + 2, 0, False, False)
            pair_steps(MPAIRS - 2, 1, False, False)
            pair_steps(MPAIRS - 1, 0, False, True)
            pe.wait_ge(h_lo_done, 2 * 4 * MPAIRS - 1)
            for r in range(4):
                down_part(4 * MPAIRS - 1, 1, 0, False, r, 0)
            pe.wait_ge(h_lo_done, 2 * 4 * MPAIRS)
            for r in range(4):
                down_part(4 * MPAIRS - 1, 1, 0, False, r, 1).then_inc(down_done, 1)


def build(nc, x_t, x_tok, w_t, b_qk, b_v, b_o, gate_q, up_q, down_q, gate_a, up_a, down_a, out):
    with nc.sbuf_tensor("y", [P, TILES * D], F32) as y, nc.sbuf_tensor("ident", [P, P], F32) as ident:
        attention_phase(nc, y, ident, x_t, x_tok, w_t, b_qk, b_v, b_o)
        ffn_phase(nc, y, ident, gate_q, up_q, down_q, gate_a, up_a, down_a, out)


def kernel(L0_attn_x, L0_attn_Wq, L0_attn_bq, L0_attn_Wk, L0_attn_bk, L0_attn_Wv, L0_attn_bv, L0_attn_Wo, L0_attn_bo,
           L0_ffn_gate_q, L0_ffn_gate_absmax, L0_ffn_up_q, L0_ffn_up_absmax, L0_ffn_down_q, L0_ffn_down_absmax):
    import concourse.bacc as bacc
    from concourse.bass_utils import run_bass_kernel_spmd

    def features(w):
        return np.asarray(w).T.reshape(KT, P, D).transpose(1, 0, 2)

    def hidden_q(q):
        return np.asarray(q).reshape(MT, P, KT, P).transpose(0, 3, 2, 1).reshape(MT, P, D)

    def hidden_a(a):
        return np.asarray(a).reshape(MT, P, KT, 2).transpose(0, 3, 2, 1).reshape(MT, 2, D)

    x = np.asarray(L0_attn_x).reshape(TILES * P, D)
    arrays = {
        "x_t": x.reshape(B, L, KT, P).transpose(0, 3, 2, 1),
        "x_tok": x.reshape(TILES, P, D).transpose(1, 0, 2),
        "w_t": np.stack([features(w) for w in (L0_attn_Wq, L0_attn_Wk, L0_attn_Wv, L0_attn_Wo)]),
        "b_qk": np.concatenate([np.asarray(b).reshape(KT, P).T for b in (L0_attn_bq, L0_attn_bk)], axis=1),
        "b_v": np.asarray(L0_attn_bv).reshape(1, D),
        "b_o": np.asarray(L0_attn_bo).reshape(1, D),
        "gate_q": hidden_q(L0_ffn_gate_q),
        "up_q": hidden_q(L0_ffn_up_q),
        "down_q": np.asarray(L0_ffn_down_q).T.reshape(MT, P, D),
        "gate_a": hidden_a(L0_ffn_gate_absmax),
        "up_a": hidden_a(L0_ffn_up_absmax),
        "down_a": np.asarray(L0_ffn_down_absmax).reshape(D, MT, 2).transpose(1, 2, 0),
    }
    arrays = {name: np.ascontiguousarray(a) for name, a in arrays.items()}
    nc = bacc.Bacc("TRN2", target_bir_lowering=False, num_devices=1)
    args = [nc.dram_tensor(name, a.shape, mybir.dt.from_np(a.dtype), kind="ExternalInput").ap()
            for name, a in arrays.items()]
    out = nc.dram_tensor("out", (TILES, P, D), F32, kind="ExternalOutput").ap()
    build(nc, *args, out)
    r = run_bass_kernel_spmd(nc, [arrays], core_ids=[0])
    return r.results[0]["out"].reshape(B, L, D)
```

```python
from contextlib import ExitStack

import numpy as np

import concourse.bass as bass
from concourse import mybir

ALU = mybir.AluOpType
ACT = mybir.ActivationFunctionType
AX_X = mybir.AxisListType.X
F32 = mybir.dt.float32
F32R = mybir.dt.float32r
F16 = mybir.dt.float16
BF16 = mybir.dt.bfloat16

P = 128
B, L, D, H = 8, 256, 512, 32
HD = D // H
M = 1792
KT = D // P
QT = L // P
TILES = B * QT
PAIRS = H // 2
GROUPS = H // 4
CAUSAL = P + L
VW = 3 * HD + 1
VS = VW + 1
PSCALE = 2048.0
BIG = 1.0e30
EPS = 1e-5

MT = M // P
MPAIRS = MT // 2
CHUNK = 4 * P
CHUNKS = TILES // 4
UNITS = 6

LEFT = [(0.30380722880363464, 1.1266505718231201), (0.1301555633544922, 0.12570475041866302),
        (0.09966795146465302, 0.01456246618181467)]
LEFT_LAST = 0.09105003625154495
RIGHT = [(0.08134990185499191, -0.0017695986898615956), (0.0918029397726059, -0.0292965117841959),
         (0.12190717458724976, -0.16882602870464325), (0.2770431637763977, -1.2163453102111816)]
LINES = LEFT + RIGHT
ZERO_CODE = 7.0

HALVES = ([("qk", n, 2) for n in range(4)] + [("o", 0, 0), ("o", 0, 1), ("qk", 4, 2), ("qk", 5, 2), ("o", 1, 0),
          ("o", 1, 1), ("qk", 6, 2), ("qk", 7, 2)] + [("v", t, half) for t in range(QT) for half in range(2)])
FILL = {s: [] for s in range(H)}
for n, task in enumerate(HALVES):
    FILL[min(2 * n + 1, 30)].append(task + (0,))
for t in range(QT):
    FILL[5 + 2 * t].append(("aT", t, 2, 1))
for g in range(PAIRS):
    FILL[min(4 + 2 * g, 31)].append(("stack", g, 2, 0 if g == 14 else 1))


def tasks_of(first, last):
    steps, before = {}, [None, None]
    for s in range(H):
        steps[s] = []
        for kind, n, half, bank in FILL[s]:
            if (kind in ("aT", "o") and first) or (kind in ("qk", "stack", "v") and last):
                continue
            steps[s].append((kind, n, half, bank, before[bank]))
            before[bank] = (kind, n)
    return steps, before


L1, R1, L2, R2, L3, R3, CODE = range(7)
DEQ = 7
ACT_STEPS = []
for u in range(UNITS):
    ACT_STEPS += [("z", u, 0)] + [("line", u, n) for n in range(6)]
    ACT_STEPS += [("high", u - 1, 0)] if u else []
    ACT_STEPS += [("line", u, 6)]


def lines_for(codes):
    if codes == 0:
        return 0
    line = (1, 4, 4, 5, 5, 6, 6)[(codes - 1) % DEQ]
    return ACT_STEPS.index(("line", (codes - 1) // DEQ, line)) + 1


def unit(u):
    return (u // 2, u % 2) if u < 4 else (u - 4, 2)


class WeightSteps:
    def __init__(self, load, line_step, high_half, code_step, scale, low_half, wt_hi, wt_lo, w_lo_done, up_done,
                 down_done):
        self.load, self.line_step, self.high_half = load, line_step, high_half
        self.code_step, self.scale, self.low_half = code_step, scale, low_half
        self.wt_hi, self.wt_lo = wt_hi, wt_lo
        self.w_lo_done, self.up_done, self.down_done = w_lo_done, up_done, down_done


def weight_steps(nc, sb, sem, wt_hi, wt_lo, gate_q, up_q, down_q, gate_a, up_a, down_a):
    codes = sb("codes", [P, 2, D], mybir.dt.int32)
    scales = sb("scales", [P, 2, D], F32)
    z = sb("z", [P, 2, D], F32)
    lines = sb("lines", [P, len(LINES), D], F32)
    left = sb("left", [P, D], F32)
    right = sb("right", [P, D], F32)
    w = sb("w", [P, 2, D], F32)

    loaded = [sem(f"f_loaded{i}") for i in range(2)]
    z_done, line_done, deq, scaled = sem("f_z_done"), sem("line_done"), sem("deq"), sem("scaled")
    w_hi_done, w_lo_done = sem("f_w_hi_done"), sem("f_w_lo_done")
    up_done, down_done = sem("up_done"), sem("down_done")

    def load(sp, pair, u, first):
        tile, matrix = unit(u)
        if not (first and u < 2):
            sp.wait_ge(z_done, 6 * pair + u - 1)
            sp.wait_ge(scaled, 6 * pair + u - 1)
        q = (gate_q, up_q, down_q)[matrix]
        a = (gate_a, up_a, down_a)[matrix]
        j = 2 * pair + tile
        sp.dma_start(codes[:, u % 2], q[bass.ds(j, 1)].rearrange("a p n -> (a p) n")).then_inc(loaded[u % 2], 16)
        for side in range(2):
            row = a[bass.ds(j, 1), side, :].to_broadcast([64, D])
            sp.dma_start(scales[64 * side:64 * side + 64, u % 2], row).then_inc(loaded[u % 2], 16)

    def line_step(act, pair, par, k, first):
        kind, u, n = ACT_STEPS[k]
        count = 6 * pair + u
        if kind == "z":
            act.wait_ge(loaded[u % 2], 48 * (3 * pair + u // 2 + 1))
            if not (first and u < 2):
                act.wait_ge(deq, DEQ * (count - 2) + L3 + 1)
            nc.scalar.activation(z[:, u % 2], codes[:, u % 2], ACT.Copy, bias=-ZERO_CODE).then_inc(z_done, 1)
        elif kind == "line":
            if n == 0:
                act.wait_ge(z_done, count + 1)
            if not (first and u == 0):
                reader = (L1, L1, L2, R1, R1, R2, R3)[n]
                act.wait_ge(deq, DEQ * (count - 1) + reader + 1)
            slope, at_zero = LINES[n]
            nc.scalar.activation(lines[:, n], z[:, u % 2], ACT.Copy, scale=slope, bias=at_zero
                                 ).then_inc(line_done, 1)
        else:
            high_half(act, pair, par, u)

    def high_half(act, pair, par, u):
        tile, matrix = unit(u)
        act.wait_ge(scaled, 6 * pair + u + 1)
        if not (isinstance(pair, int) and pair < 2):
            if matrix < 2:
                act.wait_ge(up_done, 8 * (pair - 1))
            else:
                act.wait_ge(down_done, 16 * (pair - 1))
        nc.scalar.activation(wt_hi[:, par, tile, matrix], w[:, u % 2], ACT.Copy).then_inc(w_hi_done, 1)

    def code_step(dve, pair, k, first):
        u, n = k // DEQ, k % DEQ
        count = 6 * pair + u
        before = DEQ * count
        ready = 7 * count
        if n == L1:
            dve.wait_ge(line_done, ready + 2)
            if not (first and u == 0):
                dve.wait_ge(deq, before)
            nc.vector.tensor_tensor(left[:], lines[:, 0], lines[:, 1], ALU.min).then_inc(deq, 1)
        elif n == R1:
            dve.wait_ge(line_done, ready + 5)
            nc.vector.scalar_tensor_tensor(right[:], lines[:, 3], 0.0, lines[:, 4], ALU.max,
                                           ALU.max).then_inc(deq, 1)
        elif n == L2:
            dve.wait_ge(deq, before + L1 + 1)
            nc.vector.tensor_tensor(left[:], left[:], lines[:, 2], ALU.min).then_inc(deq, 1)
        elif n == R2:
            dve.wait_ge(line_done, ready + 6)
            dve.wait_ge(deq, before + R1 + 1)
            nc.vector.tensor_tensor(right[:], right[:], lines[:, 5], ALU.max).then_inc(deq, 1)
        elif n == L3:
            dve.wait_ge(deq, before + L2 + 1)
            nc.vector.scalar_tensor_tensor(left[:], z[:, u % 2], LEFT_LAST, left[:], ALU.mult,
                                           ALU.min).then_inc(deq, 1)
        elif n == R3:
            dve.wait_ge(line_done, ready + 7)
            dve.wait_ge(deq, before + R2 + 1)
            nc.vector.tensor_tensor(right[:], right[:], lines[:, 6], ALU.max).then_inc(deq, 1)
        else:
            dve.wait_ge(deq, before + R3 + 1)
            if not (first and u < 2):
                dve.wait_ge(w_lo_done, count - 1)
            nc.vector.scalar_tensor_tensor(w[:, u % 2], left[:], 0.0, right[:], ALU.min,
                                           ALU.add).then_inc(deq, 1)

    def scale(pool, pair, u):
        pool.wait_ge(deq, DEQ * (6 * pair + u) + CODE + 1)
        pool.wait_ge(loaded[u % 2], 48 * (3 * pair + u // 2 + 1))
        nc.gpsimd.tensor_tensor(w[:, u % 2], w[:, u % 2], scales[:, u % 2], ALU.mult).then_inc(scaled, 1)

    def low_half(pool, pair, par, u):
        tile, matrix = unit(u)
        pool.wait_ge(w_hi_done, 6 * pair + u + 1)
        nc.gpsimd.tensor_tensor(wt_lo[:, par, tile, matrix], w[:, u % 2],
                                wt_hi[:, par, tile, matrix].bitcast(F32), ALU.subtract).then_inc(w_lo_done, 1)

    return WeightSteps(load, line_step, high_half, code_step, scale, low_half, wt_hi, wt_lo, w_lo_done, up_done, down_done)


EARLY = 4


def early_codes(s):
    return DEQ * EARLY * max(s - 2, 0) * (s + 20) // ((H - 2) * (H + 20))


def early_lines(s):
    return lines_for(early_codes(min(s + 1, H)))


def attention_phase(nc, block, sem, y, ident, consts, weights, projection, x_t, x_tok, w_t, b_qk, b_v, b_o):
    with ExitStack() as ctx:
        def sb(name, shape, dt):
            return ctx.enter_context(nc.sbuf_tensor(name, shape, dt))

        qkv_hi = weights.wt_hi[:].rearrange("p a t m n -> p (a t m) n").rearrange("p (w k) n -> p w k n", k=KT)
        qkv_lo = weights.wt_lo[:].rearrange("p a t m n -> p (a t m) n").rearrange("p (w k) n -> p w k n", k=KT)
        o_hi = sb("o_hi", [P, KT, D], F32R)
        o_lo = sb("o_lo", [P, KT, D], F32R)
        w_hi = [qkv_hi[:, 0], qkv_hi[:, 1], qkv_hi[:, 2], o_hi[:]]
        w_lo = [qkv_lo[:, 0], qkv_lo[:, 1], qkv_lo[:, 2], o_lo[:]]
        x_in, x_hi, x_lo, qk_hi, qk_lo, sel, bv, v_sum, v_rest = projection
        stack = sb("stack", [P, PAIRS, 2 * L], F32R)
        v_parts = sb("v_parts", [P, 2, QT, H, VW], BF16)
        mask = sb("mask", [P, L], F32)
        masked = sb("masked", [P, 2, CAUSAL], F32)
        low = sb("low", [P, 2, QT], F32)
        probs = sb("probs", [P, 2, CAUSAL], F32)
        pt_hi = sb("pt_hi", [P, 4, CAUSAL], F16)
        pt_lo = sb("pt_lo", [P, 4, CAUSAL], F16)
        att = sb("att", [P, QT, D], F32)
        at_hi = sb("at_hi", [P, QT, D], F32R)
        at_lo = sb("at_lo", [P, QT, D], F32R)
        bqk = sb("bqk", [P, 2 * KT], F32)
        bo = sb("bo", [P, D], F32)
        o_sum = sb("o_sum", [P, 8, HD], F32)
        o_inv = sb("o_inv", [P, 8], F32)
        stats = sb("stats", [P, QT, 6], F32)
        moments = sb("moments", [P, QT, 2], F32)
        rs = sb("rs", [P, 4, QT], F32)

        ps_s = [ctx.enter_context(nc.psum_tensor(f"ps_s{i}", [P, 512], F32)) for i in range(2)]
        ps_t = [ctx.enter_context(nc.psum_tensor(f"ps_t{i}", [P, 512], F32)) for i in range(2)]
        ps_o = [ctx.enter_context(nc.psum_tensor(f"ps_o{i}", [P, 512], F32)) for i in range(2)]
        ps_x = [ctx.enter_context(nc.psum_tensor(f"ps_x{i}", [P, 512], F32)) for i in range(2)]

        w_loaded = [sem(f"w_loaded{i}") for i in range(4)]
        x_loaded = sem("x_loaded")
        tok_loaded = sem("tok_loaded")
        b_loaded = sem("b_loaded")
        ident_zero, ident_done = sem("ident_zero"), sem("ident_done")
        mask_zero, mask_done = sem("mask_zero"), sem("mask_done")
        sel_zero, sel_done = sem("sel_zero"), sem("sel_done")
        ones_done, bq_done, consts_done = sem("ones_done"), sem("bq_done"), sem("consts_done")
        w_hi_done, w_lo_done = sem("w_hi_done"), sem("w_lo_done")
        x_hi_done, x_lo_done = sem("x_hi_done"), sem("x_lo_done")
        qk_done, qk_hi_done, qk_lo_done = sem("qk_done"), sem("qk_hi_done"), sem("qk_lo_done")
        stack_done, stack_copied = sem("stack_done"), sem("stack_copied")
        v_done, v_summed = sem("v_done"), sem("v_summed")
        v1_done, v_rest_done, v2_done, v3_done = sem("v1_done"), sem("v_rest_done"), sem("v2_done"), sem("v3_done")
        scores_done, masked_done, probs_done = sem("scores_done"), sem("masked_done"), sem("probs_done")
        pt_done, pt_hi_done, pt_lo_done = sem("pt_done"), sem("pt_hi_done"), sem("pt_lo_done")
        pv_done, o_inv_done, o_sum_done, att_done = sem("pv_done"), sem("o_inv_done"), sem("o_sum_done"), sem("att_done")
        at_done, at_hi_done, at_lo_done = sem("at_done"), sem("at_hi_done"), sem("at_lo_done")
        o_done, bo_added, z_done = sem("o_done"), sem("bo_added"), sem("z_done")
        stats_done, moments_done, rs_done, x1_done = sem("stats_done"), sem("moments_done"), sem("rs_done"), sem("x1_done")
        pool_step = sem("pool_step")

        stage = y[:].rearrange("p (w k n) -> p w k n", w=4, k=KT)

        def w_scale(w):
            return -1.0 / 4.0 if w == 0 else 1.0

        def evacuated(kind, n, b):
            return {"qk": (qk_lo_done, 8 * (b + 1) + n + 1), "stack": (stack_copied, 16 * (b + 1) + n + 1),
                    "v": (v_summed, 2 * (b + 1) + n + 1), "aT": (at_lo_done, 2 * (b - 1) + n + 1),
                    "o": (z_done, 2 * (b - 1) + n + 1)}[kind]

        START = [("qk", n) for n in range(4)]
        for f in range(KT):
            START += [("stack", g) for g in range(4 * f, 4 * f + 4)]
            START += [("qk", n) for n in (2 * f + 4, 2 * f + 5) if n < 2 * KT]
        START += [("v", t) for t in range(QT)]

        def projections_over(engine):
            engine.wait_ge(v_done, 2 * B)
            engine.wait_ge(v3_done, 2 * B)
            engine.wait_ge(stack_done, PAIRS * B)

        @block.sync
        def _(sp):
            sp.dma_start(x_in[:], x_t[0]).then_inc(x_loaded, 16)
            for w in range(4):
                sp.dma_start(stage[:, w], w_t[w]).then_inc(w_loaded[w], 16)
                if w == 0:
                    sp.dma_start(bqk[:], b_qk).then_inc(b_loaded, 16)
                    sp.dma_start(bv[:], b_v.to_broadcast([P, D])).then_inc(b_loaded, 16)
                    sp.dma_start(bo[:], b_o.to_broadcast([P, D])).then_inc(b_loaded, 16)
            sp.wait_ge(x_lo_done, 1)
            sp.dma_start(x_in[:], x_t[1]).then_inc(x_loaded, 16)
            sp.wait_ge(w_lo_done, 4)
            sp.dma_start(y[:].rearrange("p (t n) -> p t n", t=TILES), x_tok).then_inc(tok_loaded, 16)
            with sp.Fori(2, B) as b:
                sp.wait_ge(x_lo_done, b)
                sp.dma_start(x_in[:], x_t[bass.ds(b, 1)].rearrange("a p k n -> p (a k) n")).then_inc(x_loaded, 16)
            projections_over(sp)

        @block.gpsimd
        def _(pool):
            nc.gpsimd.memset(sel[:].bitcast(F32), 0.0).then_inc(sel_zero, 1)
            nc.gpsimd.memset(ident[:], 0.0).then_inc(ident_zero, 1)
            nc.gpsimd.memset(mask[:], 0.0).then_inc(mask_zero, 1)
            for n, value in enumerate((EPS, -0.5, 1.5, -1.0)):
                nc.gpsimd.memset(consts[:, n], value).then_inc(consts_done, 1)
            pool.wait_ge(consts_done, 4)
            nc.gpsimd.memset(v_parts[:, :, :, :, 3 * HD:VW], 1.0).then_inc(ones_done, 1)
            pool.wait_ge(sel_zero, 1)
            for kind, copies in ((0, slice(0, 4, 2)), (1, slice(1, 4, 2)), (2, slice(0, 2)), (3, slice(2, 4))):
                for pair in range(4):
                    for c in range(4)[copies]:
                        cols = sel[:, kind, pair].rearrange("p (e c d) -> p e c d", e=2, c=4)[:, :, c, :]
                        nc.gpsimd.affine_select(
                            out=cols, in_=cols.bitcast(F32), compare_op=ALU.not_equal, fill=1.0,
                            base=-32 * pair, pattern=[[-16, 2], [-1, 16]], channel_multiplier=1,
                        ).then_inc(sel_done, 1)
            pool.wait_ge(ident_zero, 1)
            nc.gpsimd.affine_select(out=ident[:], in_=ident[:], compare_op=ALU.not_equal, fill=1.0, base=0,
                                    pattern=[[-1, P]], channel_multiplier=1).then_inc(ident_done, 1)
            pool.wait_ge(mask_zero, 1)
            nc.gpsimd.affine_select(out=mask[:, P:L], in_=mask[:, P:L], compare_op=ALU.is_ge, fill=BIG, base=0,
                                    pattern=[[-1, P]], channel_multiplier=1).then_inc(mask_done, 1)
            pool.wait_ge(b_loaded, 48)

            def v_rest_step(b, par, t):
                if not (isinstance(b, int) and 2 * b + t == 0):
                    pool.wait_ge(v3_done, 2 * b + t)
                pool.wait_ge(v1_done, 2 * b + t + 1)
                nc.gpsimd.tensor_tensor(v_rest[:].rearrange("p (h d) -> p h d", h=H),
                                        v_sum[:].rearrange("p (h d) -> p h d", h=H),
                                        v_parts[:, par, t, :, 0:HD], ALU.subtract).then_inc(v_rest_done, 1)
                pool.wait_ge(v2_done, 2 * b + t + 1)
                nc.gpsimd.tensor_tensor(v_parts[:, par, t, :, 2 * HD:3 * HD],
                                        v_rest[:].rearrange("p (h d) -> p h d", h=H),
                                        v_parts[:, par, t, :, HD:2 * HD], ALU.subtract).then_inc(v3_done, 1)

            def normalise_heads(b, g):
                pool.wait_ge(o_sum_done, 8 * b + g + 1)
                if g == 0 and not (isinstance(b, int) and b == 0):
                    pool.wait_ge(at_done, 2 * b)
                out = att[:, :, 4 * g * HD:4 * (g + 1) * HD].rearrange("p t (h d) -> p t h d", h=4)
                inv = o_inv[:].rearrange("p (t h) -> p t h", t=QT).unsqueeze(3).to_broadcast([P, QT, 4, HD])
                nc.gpsimd.tensor_tensor(out, o_sum[:].rearrange("p (t h) d -> p t h d", t=QT), inv,
                                        ALU.mult).then_inc(att_done, 1)

            def add_bo(b):
                for t in range(QT):
                    cols = y[:, bass.ds((2 * b + t) * D, D)]
                    nc.gpsimd.tensor_tensor(cols, cols, bo[:], ALU.add).then_inc(bo_added, 1)

            def root(b, t):
                rstd_steps(nc, pool, moments[:, t, 1:2], rs[:, :, t:t + 1], consts, moments_done, 2 * b + t + 1, pool_step,
                           RSTD_STEPS * (2 * b + t), rs_done)

            def batch(b, par, first, last):
                for s in range(H):
                    if s == 0:
                        add_bo(b)
                    if s % 4 == 0 and s >= 8:
                        normalise_heads(b, s // 4 - 2)
                    elif s % 4 == 0 and not first:
                        normalise_heads(b - 1, GROUPS - 2 + s // 4)
                    if s == 13 and not first:
                        root(b - 1, 0)
                    if s == 21 and not first:
                        root(b - 1, 1)
                    if s in (28, 31) and not last:
                        v_rest_step(b + 1, 1 - par, (s - 28) // 3)
                    if last and s == 1:
                        projections_over(pool)
                    if last:
                        for u in range(early_codes(s) // DEQ, early_codes(s + 1) // DEQ):
                            weights.scale(pool, 0, u)
                            if u:
                                weights.low_half(pool, 0, 0, u - 1)

            pool.wait_ge(tok_loaded, 16)
            for t in range(QT):
                v_rest_step(0, 0, t)
            batch(0, 0, True, False)
            with pool.Fori(0, (B - 2) // 2) as i:
                batch(2 * i + 1, 1, False, False)
                batch(2 * i + 2, 0, False, False)
            batch(B - 1, 1, False, True)
            normalise_heads(B - 1, GROUPS - 2)
            normalise_heads(B - 1, GROUPS - 1)
            root(B - 1, 0)
            weights.low_half(pool, 0, 0, EARLY - 1)
            root(B - 1, 1)
            weights.scale(pool, 0, EARLY)

        @block.scalar
        def _(act):
            def split_x(b):
                act.wait_ge(x_loaded, 16 * b + 16)
                if not (isinstance(b, int) and b == 0):
                    act.wait_ge(v_done, 2 * b)
                nc.scalar.activation(x_hi[:], x_in[:], ACT.Copy).then_inc(x_hi_done, 1)

            def evacuate(kind, n, bank, b, par):
                if kind == "qk":
                    f, w = n // 2, n % 2
                    act.wait_ge(qk_done, 8 * b + n + 1)
                    if not (isinstance(b, int) and b == 0 and f < 2):
                        act.wait_ge(stack_done, 16 * b + 4 * (f - 2) + 4)
                    nc.scalar.activation(qk_hi[:, f % 2, w], ps_x[bank][:, 0:L], ACT.Identity,
                                         bias=bqk[:, KT * w + f:KT * w + f + 1]).then_inc(qk_hi_done, 1)
                elif kind == "stack":
                    act.wait_ge(stack_done, 16 * b + n + 1)
                    nc.scalar.activation(stack[:, n], ps_x[bank][:], ACT.Copy).then_inc(stack_copied, 1)
                elif kind == "v":
                    act.wait_ge(v_summed, 2 * b + n + 1)
                    nc.scalar.activation(v_parts[:, par, n, :, 0:HD], v_sum[:].rearrange("p (h d) -> p h d", h=H),
                                         ACT.Copy).then_inc(v1_done, 1)
                elif kind == "aT":
                    act.wait_ge(at_done, 2 * b + n + 1)
                    nc.scalar.activation(at_hi[:, n], ps_x[bank][:], ACT.Copy).then_inc(at_hi_done, 1)

            def v2_step(b, par, t):
                act.wait_ge(v_rest_done, 2 * b + t + 1)
                nc.scalar.activation(v_parts[:, par, t, :, HD:2 * HD], v_rest[:].rearrange("p (h d) -> p h d", h=H),
                                     ACT.Copy).then_inc(v2_done, 1)

            def high_halves(b, h):
                head = 32 * b + h
                act.wait_ge(pt_done, head + 1)
                if not (isinstance(head, int) and head < 4):
                    act.wait_ge(pv_done, head - 3)
                nc.scalar.activation(pt_hi[:, h % 4], ps_t[h % 2][:, 0:CAUSAL], ACT.Copy,
                                     scale=PSCALE).then_inc(pt_hi_done, 1)

            def batch(b, par, first, last):
                steps, _ = tasks_of(first, last)
                for s in range(H):
                    if s == 0 and not last:
                        split_x(b + 1)
                    if s > 1:
                        high_halves(b, s - 2)
                    elif not first:
                        high_halves(b - 1, H - 2 + s)
                    act.wait_ge(masked_done, 32 * b + s + 1)
                    if not (first and s < 2):
                        act.wait_ge(pt_done, 32 * b + s - 1)
                    for t, cols in ((0, slice(0, P)), (1, slice(P, CAUSAL))):
                        last_exp = nc.scalar.activation(probs[:, s % 2, cols], masked[:, s % 2, cols], ACT.Exp,
                                                        bias=low[:, s % 2, t:t + 1], scale=-1.0)
                    last_exp.then_inc(probs_done, 1)
                    for kind, n, half_, bank, _ in steps[s]:
                        if half_:
                            evacuate(kind, n, bank, b - 1 if kind in ("aT", "o") else b + 1,
                                     1 - par)
                    if s in (28, 31) and not last:
                        v2_step(b + 1, 1 - par, (s - 28) // 3)
                    if last and s == 1:
                        projections_over(act)
                    if last:
                        for k in range(early_lines(s), early_lines(s + 1)):
                            weights.line_step(act, 0, 0, k, True)

            for w in range(4):
                act.wait_ge(w_loaded[w], 16)
                nc.scalar.activation(w_hi[w], stage[:, w], ACT.Copy, scale=w_scale(w)).then_inc(w_hi_done, 1)
                if w == 0:
                    split_x(0)
                    act.wait_ge(b_loaded, 48)
                    nc.scalar.activation(bqk[:, 0:KT], bqk[:, 0:KT], ACT.Copy, scale=w_scale(0)).then_inc(bq_done, 1)
            act.wait_ge(bq_done, 1)
            act.wait_ge(ones_done, 1)
            for k, (kind, n) in enumerate(START):
                evacuate(kind, n, k % 2, 0, 0)
                if kind == "v":
                    v2_step(0, 0, n)
            batch(0, 0, True, False)
            with act.Fori(0, (B - 2) // 2) as i:
                batch(2 * i + 1, 1, False, False)
                batch(2 * i + 2, 0, False, False)
            batch(B - 1, 1, False, True)
            high_halves(B - 1, H - 2)
            high_halves(B - 1, H - 1)
            for t in range(QT):
                evacuate("aT", t, t, B - 1, 0)
            for k in range(early_lines(H), lines_for(DEQ * (EARLY + 1))):
                weights.line_step(act, 0, 0, k, True)

        @block.vector
        def _(dve):
            heads = dve.alloc_register("heads")
            dve.reg_mov(heads, 0)

            def split_x(b):
                dve.wait_ge(x_hi_done, b + 1)
                nc.vector.tensor_tensor(x_lo[:], x_in[:], x_hi[:].bitcast(F32), ALU.subtract).then_inc(x_lo_done, 1)

            def evacuate(kind, n, bank, b):
                if kind == "qk":
                    f, w = n // 2, n % 2
                    dve.wait_ge(qk_hi_done, 8 * b + n + 1)
                    nc.vector.scalar_tensor_tensor(
                        qk_lo[:, f % 2, w], ps_x[bank][:, 0:L], bqk[:, KT * w + f:KT * w + f + 1],
                        qk_hi[:, f % 2, w].bitcast(F32), ALU.add, ALU.subtract).then_inc(qk_lo_done, 1)
                elif kind == "v":
                    dve.wait_ge(v_done, 2 * b + n + 1)
                    if not (isinstance(b, int) and b == 0 and n == 0):
                        dve.wait_ge(v_rest_done, 2 * b + n)
                    nc.vector.tensor_tensor(v_sum[:], ps_x[bank][:], bv[:], ALU.add).then_inc(v_summed, 1)
                elif kind == "aT":
                    dve.wait_ge(at_hi_done, 2 * b + n + 1)
                    nc.vector.tensor_tensor(at_lo[:, n], ps_x[bank][:], at_hi[:, n].bitcast(F32),
                                            ALU.subtract).then_inc(at_lo_done, 1)
                elif kind == "o":
                    dve.wait_ge(o_done, 2 * b + n + 1)
                    dve.wait_ge(bo_added, 2 * b + n + 1)
                    cols = y[:, bass.ds((2 * b + n) * D, D)]
                    nc.vector.tensor_tensor(cols, ps_x[bank][:], cols, ALU.add).then_inc(z_done, 1)

            def layernorm(b, t, stage_):
                cols = y[:, bass.ds((2 * b + t) * D, D)]
                if stage_ == 0:
                    dve.wait_ge(tok_loaded, 16)
                    dve.wait_ge(z_done, 2 * b + t + 1)
                    nc.vector.bn_stats(stats[:, t], cols).then_inc(stats_done, 1)
                elif stage_ == 1:
                    dve.wait_ge(tok_loaded, 16)
                    dve.wait_ge(stats_done, 2 * b + t + 1)
                    nc.vector.bn_aggr(moments[:, t], stats[:, t]).then_inc(moments_done, 1)
                else:
                    dve.wait_ge(rs_done, 2 * b + t + 1)
                    nc.vector.tensor_scalar(cols, cols, moments[:, t, 0:1], rs[:, 3, t:t + 1], ALU.subtract,
                                            ALU.mult).then_inc(x1_done, 1)

            def sum_heads(b, g):
                dve.wait_ge(pv_done, 32 * b + 4 * g + 4)
                if not (isinstance(b, int) and b == 0 and g == 0):
                    dve.wait_ge(att_done, 8 * b + g)
                out = ps_o[g % 2][:, 0:8 * VS].rearrange("p (h c) -> p h c", c=VS)
                nc.vector.reciprocal(o_inv[:].unsqueeze(2), out[:, :, 3 * HD:VW])
                nc.vector.tensor_reduce(o_sum[:], out[:, :, 0:3 * HD].rearrange("p h (c d) -> p h d c", c=3),
                                        axis=AX_X, op=ALU.add).then_inc(o_sum_done, 1)

            def low_halves(b, h):
                dve.wait_ge(pt_hi_done, 32 * b + h + 1)
                nc.vector.scalar_tensor_tensor(pt_lo[:, h % 4], ps_t[h % 2][:, 0:CAUSAL], PSCALE, pt_hi[:, h % 4],
                                               ALU.mult, ALU.subtract).then_inc(pt_lo_done, 1)

            def batch(b, par, first, last):
                steps, _ = tasks_of(first, last)
                for s in range(H):
                    if s == 0 and not last:
                        split_x(b + 1)
                    dve.reg_add(heads, heads, 1)
                    dve.wait_ge(mask_done, 1)
                    dve.wait_ge(scores_done, heads)
                    for t, cols, part in ((0, slice(0, P), slice(P, L)), (1, slice(P, CAUSAL), slice(0, L))):
                        last_min = nc.vector.tensor_tensor_reduce(
                            out=masked[:, s % 2, cols], in0=ps_s[s % 2][:, cols], in1=mask[:, part], scale=1.0,
                            scalar=3.0e38, op0=ALU.add, op1=ALU.min, accum_out=low[:, s % 2, t:t + 1])
                    last_min.then_inc(masked_done, 1)
                    if s > 1:
                        low_halves(b, s - 2)
                    elif not first:
                        low_halves(b - 1, H - 2 + s)
                    if s % 4 == 0 and s >= 8:
                        sum_heads(b, s // 4 - 2)
                    elif s % 4 == 0 and not first:
                        sum_heads(b - 1, GROUPS - 2 + s // 4)
                    for kind, n, half_, bank, _ in steps[s]:
                        if half_:
                            evacuate(kind, n, bank, b - 1 if kind in ("aT", "o") else b + 1)
                    if s in (12, 13, 15) and not first:
                        layernorm(b - 1, 0, {12: 0, 13: 1, 15: 2}[s])
                    if s in (20, 21, 23) and not first:
                        layernorm(b - 1, 1, {20: 0, 21: 1, 23: 2}[s])
                    if last and s == 1:
                        projections_over(dve)
                    if last:
                        for k in range(early_codes(s), early_codes(s + 1)):
                            weights.code_step(dve, 0, k, True)

            for w in range(4):
                dve.wait_ge(w_hi_done, w + 1)
                nc.vector.scalar_tensor_tensor(
                    w_lo[w].rearrange("p k n -> p (k n)"), stage[:, w].rearrange("p k n -> p (k n)"), w_scale(w),
                    w_hi[w].rearrange("p k n -> p (k n)").bitcast(F32), ALU.mult, ALU.subtract,
                ).then_inc(w_lo_done, 1)
                if w == 0:
                    split_x(0)
            dve.wait_ge(bq_done, 1)
            for k, (kind, n) in enumerate(START):
                evacuate(kind, n, k % 2, 0)
            batch(0, 0, True, False)
            with dve.Fori(0, (B - 2) // 2) as i:
                batch(2 * i + 1, 1, False, False)
                batch(2 * i + 2, 0, False, False)
            batch(B - 1, 1, False, True)
            low_halves(B - 1, H - 2)
            low_halves(B - 1, H - 1)
            sum_heads(B - 1, GROUPS - 2)
            sum_heads(B - 1, GROUPS - 1)
            for t in range(QT):
                evacuate("aT", t, t, B - 1)

            def codes(first, last):
                for k in range(first, last):
                    weights.code_step(dve, 0, DEQ * EARLY + k, True)

            codes(0, 3)
            evacuate("o", 0, 0, B - 1)
            layernorm(B - 1, 0, 0)
            layernorm(B - 1, 0, 1)
            codes(3, 5)
            evacuate("o", 1, 1, B - 1)
            layernorm(B - 1, 1, 0)
            layernorm(B - 1, 1, 1)
            layernorm(B - 1, 0, 2)
            codes(5, 7)
            layernorm(B - 1, 1, 2)

        @block.tensor
        def _(pe):
            def products(out, parts, first, last):
                todo = [(s, m) for s_hi, s_lo, m_hi, m_lo in parts for s, m in ((s_hi, m_hi), (s_hi, m_lo), (s_lo, m_hi))]
                for n, (s, m) in list(enumerate(todo))[first:last]:
                    done = nc.tensor.matmul(out, s, m, start=n == 0, stop=n == len(todo) - 1)
                return done

            def task(kind, n, half_, bank, b, b_of):
                out = ps_x[bank]
                first, last = {0: (0, 6), 1: (6, 12), 2: (0, 12)}[half_]
                if kind == "qk":
                    f, w = n // 2, n % 2
                    pe.wait_ge(x_lo_done, b_of + 1)
                    cols = slice(f * P, (f + 1) * P)
                    products(out[:, 0:L], [(w_hi[w][:, k, cols], w_lo[w][:, k, cols], x_hi[:, k], x_lo[:, k])
                                           for k in range(KT)], first, last).then_inc(qk_done, 1)
                elif kind == "stack":
                    f, pair = n // 4, n % 4
                    pe.wait_ge(qk_lo_done, 8 * b_of + 2 * f + 2)
                    for w in range(2):
                        half_out = out[:, w * L:(w + 1) * L]
                        nc.tensor.matmul(half_out, sel[:, 2 * w, pair], qk_hi[:, f % 2, w], start=True, stop=False)
                        done = nc.tensor.matmul(half_out, sel[:, 2 * w + 1, pair], qk_lo[:, f % 2, w],
                                                start=False, stop=True)
                    done.then_inc(stack_done, 1)
                elif kind == "v":
                    rows = slice(n * P, (n + 1) * P)
                    done = products(out[:], [(x_hi[:, k, rows], x_lo[:, k, rows], w_hi[2][:, k], w_lo[2][:, k])
                                             for k in range(KT)], first, last)
                    if half_:
                        done.then_inc(v_done, 1)
                elif kind == "aT":
                    pe.wait_ge(att_done, 8 * b_of + 8)
                    for f in range(KT):
                        done = nc.tensor.transpose(out[:, f * P:(f + 1) * P], att[:, n, f * P:(f + 1) * P], ident[:])
                    done.then_inc(at_done, 1)
                elif kind == "o":
                    pe.wait_ge(at_lo_done, 2 * b_of + n + 1)
                    done = products(out[:], [(at_hi[:, n, f * P:(f + 1) * P], at_lo[:, n, f * P:(f + 1) * P],
                                              w_hi[3][:, f], w_lo[3][:, f]) for f in range(KT)], first, last)
                    if half_:
                        done.then_inc(o_done, 1)

            def transpose_probs(head, ring):
                pe.wait_ge(probs_done, head + 1)
                if not (isinstance(head, int) and head < 2):
                    pe.wait_ge(pt_lo_done, head - 1)
                for c in range(3):
                    done = nc.tensor.transpose(ps_t[ring][:, c * P:(c + 1) * P], probs[:, ring, c * P:(c + 1) * P],
                                               ident[:])
                done.then_inc(pt_done, 1)

            def values(b, par, h):
                g, j = h // 4, h % 4
                pe.wait_ge(pt_lo_done, 32 * b + h + 1)
                if h == 0:
                    pe.wait_ge(v3_done, 2 * b + 2)
                if j == 0 and not (isinstance(b, int) and b == 0 and g < 2):
                    pe.wait_ge(o_sum_done, 8 * b + g - 1)
                for t, blocks in ((0, ((0, 0),)), (1, ((1, 0), (2, 1)))):
                    out = ps_o[g % 2][:, (4 * t + j) * VS:(4 * t + j) * VS + VW]
                    todo = [(pt, c, k) for c, k in blocks for pt in (pt_hi, pt_lo)]
                    for n, (pt, c, k) in enumerate(todo):
                        done = nc.tensor.matmul(out, pt[:, j, c * P:(c + 1) * P], v_parts[:, par, k, h],
                                                start=n == 0, stop=n == len(todo) - 1)
                done.then_inc(pv_done, 1)

            def fill(tasks, b, first):
                for kind, n, half_, bank, before in tasks:
                    if half_ != 1:
                        if before:
                            pe.wait_ge(*evacuated(*before, b))
                        else:
                            pe.wait_ge(*last_evacuated(b, bank, first))
                    task(kind, n, half_, bank, b, b - 1 if kind in ("aT", "o") else b + 1)

            def batch(b, par, first, last):
                steps, _ = tasks_of(first, last)
                for s in range(H):
                    g, rows = s // 2, slice(64 * (s % 2), 64 * (s % 2) + 64)
                    if not (first and s < 2):
                        transpose_probs(32 * b + s - 2, s % 2)
                    if s % 2 == 0:
                        pe.wait_ge(stack_copied, 16 * b + g + 1)
                    if not (first and s < 2):
                        pe.wait_ge(masked_done, 32 * b + s - 1)
                    for t in (1, 0):
                        done = nc.tensor.matmul(ps_s[s % 2][:, t * P:t * P + (t + 1) * P],
                                                stack[rows, g, t * P:(t + 1) * P],
                                                stack[rows, g, L:L + (t + 1) * P], start=True, stop=True)
                    done.then_inc(scores_done, 1)
                    if s > 3:
                        values(b, par, s - 4)
                    elif not first:
                        values(b - 1, 1 - par, H - 4 + s)
                    fill(steps[s], b, first)

            def last_evacuated(b, bank, first):
                kind, n = START[-2:][bank] if first else tasks_of(False, False)[1][bank]
                return evacuated(kind, n, b - 1)

            pe.wait_ge(sel_done, 32)
            pe.wait_ge(ident_done, 1)
            pe.wait_ge(w_lo_done, 2)
            for k, (kind, n) in enumerate(START):
                if kind == "v" and n == 0:
                    pe.wait_ge(w_lo_done, 4)
                if k >= 2:
                    pe.wait_ge(*evacuated(*START[k - 2], -1))
                task(kind, n, 2, k % 2, -1, 0)
            batch(0, 0, True, False)
            with pe.Fori(0, (B - 2) // 2) as i:
                batch(2 * i + 1, 1, False, False)
                batch(2 * i + 2, 0, False, False)
            batch(B - 1, 1, False, True)
            transpose_probs(32 * B - 2, 0)
            transpose_probs(32 * B - 1, 1)
            for h in range(H - 4, H):
                values(B - 1, 1, h)
            for t in range(QT):
                pe.wait_ge(z_done, 2 * (B - 2) + t + 1)
                task("aT", t, 2, t, B, B - 1)
            for t in range(QT):
                pe.wait_ge(at_lo_done, 2 * (B - 1) + t + 1)
                task("o", t, 2, t, B, B - 1)
            pe.wait_ge(x1_done, TILES)


def rstd_steps(nc, pool, variance, rs, consts, ready, count, steps, steps_before, done):
    n = variance.shape[1]
    pool.wait_ge(ready, count)
    nc.gpsimd.tensor_tensor(rs[:, 0], variance, consts[:, 0, 0:n], ALU.add).then_inc(steps, 1)
    pool.wait_ge(steps, steps_before + 1)
    nc.gpsimd.tensor_tensor(rs[:, 1], rs[:, 0], consts[:, 1, 0:n], ALU.pow).then_inc(steps, 1)
    pool.wait_ge(steps, steps_before + 2)
    nc.gpsimd.tensor_tensor(rs[:, 2], rs[:, 1], rs[:, 1], ALU.mult).then_inc(steps, 1)
    pool.wait_ge(steps, steps_before + 3)
    nc.gpsimd.tensor_tensor(rs[:, 2], rs[:, 2], rs[:, 0], ALU.mult).then_inc(steps, 1)
    pool.wait_ge(steps, steps_before + 4)
    nc.gpsimd.tensor_tensor(rs[:, 2], rs[:, 2], consts[:, 1, 0:n], ALU.mult).then_inc(steps, 1)
    pool.wait_ge(steps, steps_before + 5)
    nc.gpsimd.tensor_tensor(rs[:, 2], rs[:, 2], consts[:, 2, 0:n], ALU.add).then_inc(steps, 1)
    pool.wait_ge(steps, steps_before + 6)
    nc.gpsimd.tensor_tensor(rs[:, 3], rs[:, 1], rs[:, 2], ALU.mult).then_inc(done, 1)


RSTD_STEPS = 6


def ffn_phase(nc, block, sem, y, ident, consts, weights, out):
    with ExitStack() as ctx:
        def sb(name, shape, dt):
            return ctx.enter_context(nc.sbuf_tensor(name, shape, dt))

        xt_hi = sb("xt_hi", [P, KT, TILES * P], F32R)
        xt_lo = sb("xt_lo", [P, KT, TILES * P], F32R)
        h_hi = sb("h_hi", [P, 2, 2, CHUNK], F32R)
        h_lo = sb("h_lo", [P, 2, 2, CHUNK], F32R)
        silu_g = sb("silu_g", [P, 2, CHUNK], F32)
        hid = sb("hid", [P, 2, CHUNK], F32)
        stats = sb("f_stats", [P, TILES, 6], F32)
        moments = sb("f_moments", [P, TILES, 2], F32)
        rs = sb("f_rs", [P, 4, TILES], F32)
        shift = sb("shift", [P, TILES], F32)

        ps_g = [ctx.enter_context(nc.psum_tensor(f"ps_g{i}", [P, 512], F32)) for i in range(2)]
        ps_u = [ctx.enter_context(nc.psum_tensor(f"ps_u{i}", [P, 512], F32)) for i in range(2)]
        ps_y = [ctx.enter_context(nc.psum_tensor(f"ps_y{i}", [P, 512], F32)) for i in range(4)]

        xt_done, xt_hi_done, xt_lo_done = sem("xt_done"), sem("xt_hi_done"), sem("xt_lo_done")
        gate_done, silu_done = sem("gate_done"), sem("silu_done")
        hid_done, h_hi_done, h_lo_done = sem("hid_done"), sem("h_hi_done"), sem("h_lo_done")
        added = sem("added")
        negated, shift_done = sem("negated"), sem("shift_done")
        stats_done, moments_done, rs_done, pool_step, norm_done, stored = (
            sem("f_stats_done"), sem("f_moments_done"), sem("f_rs_done"), sem("f_pool_step"), sem("norm_done"),
            sem("stored"))

        wt_hi, wt_lo, w_lo_done = weights.wt_hi, weights.wt_lo, weights.w_lo_done
        up_done, down_done = weights.up_done, weights.down_done

        SLOTS = 3 * CHUNKS
        NORMS = [range(0, 4), range(4, 8), range(8, 12), range(12, 14), range(14, 15), range(15, 16)]

        def codes_by(slot, first):
            late = 2 if first else 0
            return DEQ * UNITS * max(slot - late, 0) // (SLOTS - late)

        def lines_by(slot, first):
            return lines_for(codes_by(min(slot + 1, SLOTS), first)) if slot else 0

        @block.sync
        def _(sp):
            for u in range(UNITS):
                weights.load(sp, 0, u, True)
            with sp.Fori(1, MPAIRS) as pair:
                for u in range(UNITS):
                    weights.load(sp, pair, u, False)
            for t in range(TILES):
                sp.wait_ge(norm_done, t + 1)
                sp.dma_start(out[t], y[:, t * D:(t + 1) * D]).then_inc(stored, 16)
            sp.wait_ge(stored, 16 * TILES)

        @block.gpsimd
        def _(pool):
            def prepare(pair, par):
                for u in range(UNITS):
                    weights.scale(pool, pair, u)
                    if u:
                        weights.low_half(pool, pair, par, u - 1)
                weights.low_half(pool, pair, par, UNITS - 1)

            weights.scale(pool, 0, UNITS - 1)
            weights.low_half(pool, 0, 0, UNITS - 2)
            weights.low_half(pool, 0, 0, UNITS - 1)
            with pool.Fori(0, (MPAIRS - 1) // 2) as i:
                prepare(2 * i + 1, 1)
                prepare(2 * i + 2, 0)
            for n, group in enumerate(NORMS):
                tiles = slice(group.start, group.stop)
                rstd_steps(nc, pool, moments[:, tiles, 1], rs[:, :, tiles], consts, moments_done, group.stop, pool_step,
                           RSTD_STEPS * n, rs_done)
                nc.gpsimd.tensor_tensor(shift[:, tiles], moments[:, tiles, 0], consts[:, 3, 0:len(group)],
                                        ALU.mult).then_inc(negated, 1)
                pool.wait_ge(negated, n + 1)
                pool.wait_ge(rs_done, n + 1)
                nc.gpsimd.tensor_tensor(shift[:, tiles], shift[:, tiles], rs[:, 3, tiles],
                                        ALU.mult).then_inc(shift_done, 1)

        @block.scalar
        def _(act):
            def transposed(c):
                for n in range(KT * c, KT * (c + 1)):
                    act.wait_ge(xt_done, n + 1)
                    nc.scalar.activation(xt_hi[:, n % KT, c * CHUNK:(c + 1) * CHUNK], ps_y[n % 4][:],
                                         ACT.Copy).then_inc(xt_hi_done, 1)

            def hidden(step, par, tile, first):
                count = 2 * step + tile
                act.wait_ge(gate_done, count + 1)
                if not (first and step == 0):
                    act.wait_ge(hid_done, count - 1)
                nc.scalar.activation(silu_g[:, tile], ps_g[tile][:], ACT.Silu).then_inc(silu_done, 1)

            def high_half(step, par, tile, first):
                count = 2 * step + tile
                act.wait_ge(hid_done, count + 1)
                if not (first and step < 2):
                    act.wait_ge(down_done, 4 * (step - 1))
                nc.scalar.activation(h_hi[:, par, tile], hid[:, tile], ACT.Copy).then_inc(h_hi_done, 1)

            def normalise(t):
                cols = y[:, t * D:(t + 1) * D]
                act.wait_ge(shift_done, [t in group for group in NORMS].index(True) + 1)
                nc.scalar.activation(cols, cols, ACT.Identity, bias=shift[:, t:t + 1],
                                     scale=rs[:, 3, t:t + 1]).then_inc(norm_done, 1)

            def pair_steps(pair, par, first, last):
                def dequant(slot):
                    if not last:
                        for k in range(lines_by(slot, first), lines_by(slot + 1, first)):
                            weights.line_step(act, pair + 1, 1 - par, k, False)

                for c in range(CHUNKS):
                    step = 4 * pair + c
                    dequant(3 * c)
                    hidden(step, c % 2, 0, first)
                    if first and c < 2:
                        transposed(2 * c + 1)
                    if first and c == 0:
                        weights.high_half(act, 0, 0, UNITS - 1)
                    dequant(3 * c + 1)
                    high_half(step, c % 2, 0, first)
                    hidden(step, c % 2, 1, first)
                    if first and c == 0:
                        transposed(2)
                    dequant(3 * c + 2)
                    high_half(step, c % 2, 1, first)
                    if last and c >= 2:
                        for t in range(4 * (c - 2), 4 * (c - 1)):
                            normalise(t)
                if not last:
                    weights.high_half(act, pair + 1, 1 - par, UNITS - 1)

            transposed(0)
            for k in range(lines_for(DEQ * (EARLY + 1)), len(ACT_STEPS)):
                weights.line_step(act, 0, 0, k, True)
            pair_steps(0, 0, True, False)
            with act.Fori(0, (MPAIRS - 3) // 2) as i:
                pair_steps(2 * i + 1, 1, False, False)
                pair_steps(2 * i + 2, 0, False, False)
            pair_steps(MPAIRS - 2, 1, False, False)
            pair_steps(MPAIRS - 1, 0, False, True)
            for t in range(TILES // 2, TILES):
                normalise(t)

        @block.vector
        def _(dve):
            def transposed(c):
                for n in range(KT * c, KT * (c + 1)):
                    cols = slice(c * CHUNK, (c + 1) * CHUNK)
                    dve.wait_ge(xt_hi_done, n + 1)
                    nc.vector.tensor_tensor(xt_lo[:, n % KT, cols], ps_y[n % 4][:], xt_hi[:, n % KT, cols].bitcast(F32),
                                            ALU.subtract).then_inc(xt_lo_done, 1)

            def hidden(step, par, tile, first):
                count = 2 * step + tile
                dve.wait_ge(up_done, count + 1)
                dve.wait_ge(silu_done, count + 1)
                if not (first and step == 0):
                    dve.wait_ge(h_lo_done, count - 1)
                nc.vector.tensor_tensor(hid[:, tile], ps_u[tile][:], silu_g[:, tile], ALU.mult).then_inc(hid_done, 1)

            def low_half(step, par, tile):
                dve.wait_ge(h_hi_done, 2 * step + tile + 1)
                nc.vector.tensor_tensor(h_lo[:, par, tile], hid[:, tile], h_hi[:, par, tile].bitcast(F32),
                                        ALU.subtract).then_inc(h_lo_done, 1)

            def add(step, c, r):
                cols = y[:, (4 * c + r) * D:(4 * c + r + 1) * D]
                dve.wait_ge(down_done, 4 * step + r + 1)
                nc.vector.tensor_tensor(cols, ps_y[r][:], cols, ALU.add).then_inc(added, 1)

            def measure(t):
                dve.wait_ge(added, 4 * (4 * (MPAIRS - 1)) + t + 1)
                nc.vector.bn_stats(stats[:, t], y[:, t * D:(t + 1) * D]).then_inc(stats_done, 1)
                dve.wait_ge(stats_done, t + 1)
                nc.vector.bn_aggr(moments[:, t], stats[:, t]).then_inc(moments_done, 1)

            def pair_steps(pair, par, first, last):
                def dequant(slot):
                    if not last:
                        for k in range(codes_by(slot, first), codes_by(slot + 1, first)):
                            weights.code_step(dve, pair + 1, k, False)

                for c in range(CHUNKS):
                    step = 4 * pair + c
                    if not (first and c < 2):
                        for r in range(4):
                            add(step - 2, (c - 2) % 4, r)
                    dequant(3 * c)
                    hidden(step, c % 2, 0, first)
                    if first and c < 2:
                        transposed(2 * c + 1)
                    if last and c >= 2:
                        for t in range(4 * (c - 2), 4 * (c - 1)):
                            measure(t)
                    dequant(3 * c + 1)
                    low_half(step, c % 2, 0)
                    hidden(step, c % 2, 1, first)
                    if first and c == 0:
                        transposed(2)
                    dequant(3 * c + 2)
                    low_half(step, c % 2, 1)

            transposed(0)
            for k in range(DEQ * (EARLY + 1), DEQ * UNITS):
                weights.code_step(dve, 0, k, True)
            pair_steps(0, 0, True, False)
            with dve.Fori(0, (MPAIRS - 3) // 2) as i:
                pair_steps(2 * i + 1, 1, False, False)
                pair_steps(2 * i + 2, 0, False, False)
            pair_steps(MPAIRS - 2, 1, False, False)
            pair_steps(MPAIRS - 1, 0, False, True)
            for c in range(2, 4):
                for r in range(4):
                    t = 4 * c + r
                    add(4 * (MPAIRS - 1) + c, c, r)
                    measure(t)

        @block.tensor
        def _(pe):
            def gate_up(step, par, tile, c, first):
                count = 2 * step + tile
                if not (first and step == 0):
                    pe.wait_ge(hid_done, count - 1)
                cols = slice(c * CHUNK, (c + 1) * CHUNK)
                for matrix, bank, done_sem in ((0, ps_g[tile], gate_done), (1, ps_u[tile], up_done)):
                    n = 0
                    for k in range(KT):
                        hi = wt_hi[:, par, tile, matrix, k * P:(k + 1) * P]
                        lo = wt_lo[:, par, tile, matrix, k * P:(k + 1) * P]
                        for s, m in ((hi, xt_hi), (hi, xt_lo), (lo, xt_hi)):
                            done = nc.tensor.matmul(bank[:], s, m[:, k, cols], start=n == 0, stop=n == 3 * KT - 1)
                            n += 1
                    done.then_inc(done_sem, 1)

            def down(step, par, w_par, first):
                pe.wait_ge(h_lo_done, 2 * step + 2)
                for r in range(4):
                    if first:
                        pe.wait_ge(xt_lo_done, KT * CHUNKS)
                    else:
                        pe.wait_ge(added, 4 * (step - 1) + r + 1)
                    rows = slice(r * P, (r + 1) * P)
                    n = 0
                    for tile in range(2):
                        w_hi, w_lo = wt_hi[:, w_par, tile, 2], wt_lo[:, w_par, tile, 2]
                        for s, m in ((h_hi, w_hi), (h_hi, w_lo), (h_lo, w_hi)):
                            done = nc.tensor.matmul(ps_y[r][:], s[:, par, tile, rows], m, start=n == 0, stop=n == 5)
                            n += 1
                    done.then_inc(down_done, 1)

            def transposed(c):
                for n in range(KT * c, KT * (c + 1)):
                    if n >= 4:
                        pe.wait_ge(xt_lo_done, n - 3)
                    for r in range(4):
                        t = 4 * c + r
                        done = nc.tensor.transpose(ps_y[n % 4][:, r * P:(r + 1) * P],
                                                   y[:, t * D + (n % KT) * P:t * D + (n % KT + 1) * P], ident[:])
                    done.then_inc(xt_done, 1)

            def pair_steps(pair, par, first, last):
                for c in range(CHUNKS):
                    step = 4 * pair + c
                    for tile in range(2):
                        if c == 0:
                            pe.wait_ge(w_lo_done, 6 * pair + 2 * tile + 2)
                        if first and tile == 0:
                            pe.wait_ge(xt_lo_done, KT * (c + 1))
                        gate_up(step, par, tile, c, first)
                        if first and 2 * c + tile < 3:
                            transposed(2 * c + tile + 1)
                    if c == 1:
                        pe.wait_ge(w_lo_done, 6 * pair + 6)
                    if not (first and c == 0):
                        down(step - 1, (c - 1) % 2, par if c else 1 - par, first and c == 1)

            transposed(0)
            pair_steps(0, 0, True, False)
            with pe.Fori(0, (MPAIRS - 3) // 2) as i:
                pair_steps(2 * i + 1, 1, False, False)
                pair_steps(2 * i + 2, 0, False, False)
            pair_steps(MPAIRS - 2, 1, False, False)
            pair_steps(MPAIRS - 1, 0, False, True)
            down(4 * MPAIRS - 1, 1, 0, False)


def build(nc, x_t, x_tok, w_t, b_qk, b_v, b_o, gate_q, up_q, down_q, gate_a, up_a, down_a, out):
    with ExitStack() as ctx:
        def sb(name, shape, dt, ctx=ctx):
            return ctx.enter_context(nc.sbuf_tensor(name, shape, dt))

        def sem(name):
            return ctx.enter_context(nc.semaphore(name))

        y = sb("y", [P, TILES * D], F32)
        ident = sb("ident", [P, P], F32)
        consts = sb("consts", [P, 4, 4], F32)
        wt_hi = sb("wt_hi", [P, 2, 2, 3, D], F32R)
        wt_lo = sb("wt_lo", [P, 2, 2, 3, D], F32R)
        with ExitStack() as early:
            projection = [
                sb("x_in", [P, KT, L], F32, early),
                sb("x_hi", [P, KT, L], F32R, early),
                sb("x_lo", [P, KT, L], F32R, early),
                sb("qk_hi", [P, 2, 2, L], F32R, early),
                sb("qk_lo", [P, 2, 2, L], F32R, early),
                sb("sel", [P, 4, 4, P], F32R, early),
                sb("bv", [P, D], F32, early),
                sb("v_sum", [P, D], F32, early),
                sb("v_rest", [P, D], F32, early),
            ]
        weights = weight_steps(nc, sb, sem, wt_hi, wt_lo, gate_q, up_q, down_q, gate_a, up_a, down_a)
        block = ctx.enter_context(nc.Block())
        attention_phase(nc, block, sem, y, ident, consts, weights, projection, x_t, x_tok, w_t, b_qk, b_v, b_o)
        ffn_phase(nc, block, sem, y, ident, consts, weights, out)


def kernel(L0_attn_x, L0_attn_Wq, L0_attn_bq, L0_attn_Wk, L0_attn_bk, L0_attn_Wv, L0_attn_bv, L0_attn_Wo, L0_attn_bo,
           L0_ffn_gate_q, L0_ffn_gate_absmax, L0_ffn_up_q, L0_ffn_up_absmax, L0_ffn_down_q, L0_ffn_down_absmax):
    import concourse.bacc as bacc
    from concourse.bass_utils import run_bass_kernel_spmd

    def features(w):
        return np.asarray(w).T.reshape(KT, P, D).transpose(1, 0, 2)

    def hidden_q(q):
        return np.asarray(q).reshape(MT, P, KT, P).transpose(0, 3, 2, 1).reshape(MT, P, D)

    def hidden_a(a):
        return np.asarray(a).reshape(MT, P, KT, 2).transpose(0, 3, 2, 1).reshape(MT, 2, D)

    x = np.asarray(L0_attn_x).reshape(TILES * P, D)
    arrays = {
        "x_t": x.reshape(B, L, KT, P).transpose(0, 3, 2, 1),
        "x_tok": x.reshape(TILES, P, D).transpose(1, 0, 2),
        "w_t": np.stack([features(w) for w in (L0_attn_Wq, L0_attn_Wk, L0_attn_Wv, L0_attn_Wo)]),
        "b_qk": np.concatenate([np.asarray(b).reshape(KT, P).T for b in (L0_attn_bq, L0_attn_bk)], axis=1),
        "b_v": np.asarray(L0_attn_bv).reshape(1, D),
        "b_o": np.asarray(L0_attn_bo).reshape(1, D),
        "gate_q": hidden_q(L0_ffn_gate_q),
        "up_q": hidden_q(L0_ffn_up_q),
        "down_q": np.asarray(L0_ffn_down_q).T.reshape(MT, P, D),
        "gate_a": hidden_a(L0_ffn_gate_absmax),
        "up_a": hidden_a(L0_ffn_up_absmax),
        "down_a": np.asarray(L0_ffn_down_absmax).reshape(D, MT, 2).transpose(1, 2, 0),
    }
    arrays = {name: np.ascontiguousarray(a) for name, a in arrays.items()}
    nc = bacc.Bacc("TRN2", target_bir_lowering=False, num_devices=1)
    args = [nc.dram_tensor(name, a.shape, mybir.dt.from_np(a.dtype), kind="ExternalInput").ap()
            for name, a in arrays.items()]
    out = nc.dram_tensor("out", (TILES, P, D), F32, kind="ExternalOutput").ap()
    build(nc, *args, out)
    r = run_bass_kernel_spmd(nc, [arrays], core_ids=[0])
    return r.results[0]["out"].reshape(B, L, D)
```
